# Optimizing a Trainium2 kernel written in Bass

```python
import numpy as np
import jax
import jax.numpy as jnp

def _softmax(x, axis=-1):
    return jax.nn.softmax(x, axis=axis)

def _gelu(x):
    return jax.nn.gelu(x, approximate=True)

def _silu(x):
    return jax.nn.silu(x)

def _sigmoid(x):
    return jax.nn.sigmoid(x)

def _layernorm(x, axis=-1, eps=1e-05):
    m = jnp.mean(x, axis=axis, keepdims=True)
    v = jnp.var(x, axis=axis, keepdims=True)
    return (x - m) / jnp.sqrt(v + eps)

def _scatter_add(tgt, idx, src, axis=0):
    return tgt.at[idx].add(src)

def _segment_sum(src, seg, n):
    return jax.ops.segment_sum(src, seg, n)
kernel_name = 'mk_vit_tower_d1_tok_img1024_r4_d382f7'

def setup_inputs(seed: int=0):
    np.random.seed(seed)
    _w = jnp.asarray

    def _rec_inputs():
        import jax
        import jax.numpy as jnp
        _rk = jax.random.key(seed)
        x = -0.00016672 + 0.999947 * jax.random.normal(jax.random.fold_in(_rk, 1), (16, 3, 96, 96), jnp.float32)
        return x
    x = _rec_inputs()

    def _L0_tok_setup():
        import jax, jax.numpy as jnp
        import numpy as np
        IMG = 96
        P = 16
        C = 3
        D = 256
        B = 64
        key = jax.random.key(seed)
        kx, kw, kb = jax.random.split(key, 3)
        fan_in = C * P * P
        bound = 1.0 / np.sqrt(fan_in)
        x = jax.random.normal(kx, (B, C, IMG, IMG), dtype=jnp.float32)
        W = jax.random.uniform(kw, (D, fan_in), dtype=jnp.float32, minval=-bound, maxval=bound)
        b = jax.random.uniform(kb, (D,), dtype=jnp.float32, minval=-bound, maxval=bound)
        return {'x': x, 'W': W, 'b': b}
    _L0_tok_all = _L0_tok_setup()
    _L0_tok_in = {k: v for k, v in _L0_tok_all.items() if k in ('W', 'b')}
    del _L0_tok_all

    def _L0_attn_setup():
        import jax, jax.numpy as jnp
        import numpy as np
        import math
        B, T, C = (8, 512, 256)
        DIM_ATT, DIM_FFN = (256, 1024)
        N_LAYER, LAYER_ID = (12, 1)
        EPS = 1e-05

        def layer_norm(x, w, b):
            mu = jnp.mean(x, axis=-1, keepdims=True)
            var = jnp.mean(jnp.square(x - mu), axis=-1, keepdims=True)
            return (x - mu) * jax.lax.rsqrt(var + EPS) * w + b

        def time_shift(x):
            return jnp.pad(x, ((0, 0), (1, 0), (0, 0)))[:, :-1, :]

        def wkv(time_decay, time_first, k, v):
            w = -jnp.exp(time_decay)
            u = time_first

            def step(carry, kv_t):
                aa, bb, pp = carry
                kt, vt = kv_t
                ww = u + kt
                qq = jnp.maximum(pp, ww)
                e1 = jnp.exp(pp - qq)
                e2 = jnp.exp(ww - qq)
                y = (e1 * aa + e2 * vt) / (e1 * bb + e2)
                ww2 = pp + w
                qq2 = jnp.maximum(ww2, kt)
                e1b = jnp.exp(ww2 - qq2)
                e2b = jnp.exp(kt - qq2)
                return ((e1b * aa + e2b * vt, e1b * bb + e2b, qq2), y)
            init = (jnp.zeros_like(k[:, 0]), jnp.zeros_like(k[:, 0]), jnp.full_like(k[:, 0], -1e+38))
            kT = jnp.swapaxes(k, 0, 1)
            vT = jnp.swapaxes(v, 0, 1)
            _, yT = jax.lax.scan(step, init, (kT, vT))
            return jnp.swapaxes(yT, 0, 1)
        key = jax.random.key(seed)
        ks = jax.random.split(key, 16)
        r01 = LAYER_ID / (N_LAYER - 1)
        r1a0 = 1.0 - LAYER_ID / N_LAYER
        ddd = (np.arange(C, dtype=np.float32) / C)[None, None, :]
        decay_speed = -5.0 + 8.0 * (np.arange(DIM_ATT, dtype=np.float32) / (DIM_ATT - 1)) ** (0.7 + 1.3 * r01)
        zigzag = np.array([(i + 1) % 3 - 1 for i in range(DIM_ATT)], dtype=np.float32) * 0.5

        def lin(k, out_d, in_d):
            return jax.random.normal(k, (out_d, in_d), jnp.float32) * (1.0 / math.sqrt(in_d))
        return {'x': jax.random.normal(ks[0], (B, T, C), jnp.float32), 'ln1_w': jnp.ones((C,), jnp.float32), 'ln1_b': jnp.zeros((C,), jnp.float32), 'ln2_w': jnp.ones((C,), jnp.float32), 'ln2_b': jnp.zeros((C,), jnp.float32), 'att_tmk': jnp.asarray(ddd ** r1a0), 'att_tmv': jnp.asarray(ddd ** r1a0 + 0.3 * r01), 'att_tmr': jnp.asarray(ddd ** (0.5 * r1a0)), 'time_decay': jnp.asarray(decay_speed), 'time_first': jnp.asarray(np.full(DIM_ATT, math.log(0.3), np.float32) + zigzag), 'Wk': lin(ks[1], DIM_ATT, C), 'Wv': lin(ks[2], DIM_ATT, C), 'Wr': lin(ks[3], DIM_ATT, C), 'Wo': lin(ks[4], C, DIM_ATT), 'ffn_tmk': jnp.asarray(ddd ** r1a0), 'ffn_tmr': jnp.asarray(ddd ** r1a0), 'Wkey': lin(ks[5], DIM_FFN, C), 'Wrec': lin(ks[6], C, C), 'Wval': lin(ks[7], C, DIM_FFN)}
    _L0_attn_all = _L0_attn_setup()
    _L0_attn_in = {k: v for k, v in _L0_attn_all.items() if k in ('ln1_w', 'ln1_b', 'ln2_w', 'ln2_b', 'att_tmk', 'att_tmv', 'att_tmr', 'time_decay', 'time_first', 'Wk', 'Wv', 'Wr', 'Wo', 'ffn_tmk', 'ffn_tmr', 'Wkey', 'Wrec', 'Wval')}
    del _L0_attn_all

    def _L0_ffn_setup():
        import jax, jax.numpy as jnp
        import numpy as np
        BLOCK = 32
        W_BITS = 4
        ACT_BITS = 16

        def act_qdq(x):
            qmax = 2.0 ** (ACT_BITS - 1) - 1.0
            scale = jnp.maximum(jnp.max(jnp.abs(x)) / qmax, 1e-12)
            return jnp.clip(jnp.round(x / scale), -qmax - 1.0, qmax) * scale

        def fixed_qdq_u16(x):
            scale = 1.0 / 65536.0
            return jnp.clip(jnp.round(x / scale), 0.0, 65535.0) * scale

        def lpbq_dequant(w):
            O, I = w.shape
            qmax = 2.0 ** (W_BITS - 1) - 1.0
            wb = w.reshape(O, I // BLOCK, BLOCK)
            s = jnp.maximum(jnp.max(jnp.abs(wb), axis=-1, keepdims=True) / qmax, 1e-12)
            wq = jnp.clip(jnp.round(wb / s), -qmax - 1.0, qmax) * s
            return wq.reshape(O, I)
        key = jax.random.key(seed)
        k1, k2, k3, k4 = jax.random.split(key, 4)
        B, S, H, I = (2, 1024, 256, 768)
        x = jax.random.normal(k1, (B, S, H), jnp.float32)
        w_gate = jax.random.normal(k2, (I, H), jnp.float32) * 0.02
        w_up = jax.random.normal(k3, (I, H), jnp.float32) * 0.02
        w_down = jax.random.normal(k4, (H, I), jnp.float32) * 0.02
        return {'x': x, 'w_gate': w_gate, 'w_up': w_up, 'w_down': w_down}
    _L0_ffn_all = _L0_ffn_setup()
    _L0_ffn_in = {k: v for k, v in _L0_ffn_all.items() if k in ('w_gate', 'w_up', 'w_down')}
    del _L0_ffn_all
    return {'x': x, 'L0_tok_W': _L0_tok_in['W'], 'L0_tok_b': _L0_tok_in['b'], 'L0_attn_ln1_w': _L0_attn_in['ln1_w'], 'L0_attn_ln1_b': _L0_attn_in['ln1_b'], 'L0_attn_ln2_w': _L0_attn_in['ln2_w'], 'L0_attn_ln2_b': _L0_attn_in['ln2_b'], 'L0_attn_att_tmk': _L0_attn_in['att_tmk'], 'L0_attn_att_tmv': _L0_attn_in['att_tmv'], 'L0_attn_att_tmr': _L0_attn_in['att_tmr'], 'L0_attn_time_decay': _L0_attn_in['time_decay'], 'L0_attn_time_first': _L0_attn_in['time_first'], 'L0_attn_Wk': _L0_attn_in['Wk'], 'L0_attn_Wv': _L0_attn_in['Wv'], 'L0_attn_Wr': _L0_attn_in['Wr'], 'L0_attn_Wo': _L0_attn_in['Wo'], 'L0_attn_ffn_tmk': _L0_attn_in['ffn_tmk'], 'L0_attn_ffn_tmr': _L0_attn_in['ffn_tmr'], 'L0_attn_Wkey': _L0_attn_in['Wkey'], 'L0_attn_Wrec': _L0_attn_in['Wrec'], 'L0_attn_Wval': _L0_attn_in['Wval'], 'L0_ffn_w_gate': _L0_ffn_in['w_gate'], 'L0_ffn_w_up': _L0_ffn_in['w_up'], 'L0_ffn_w_down': _L0_ffn_in['w_down']}

def reference(x, L0_tok_W, L0_tok_b, L0_attn_ln1_w, L0_attn_ln1_b, L0_attn_ln2_w, L0_attn_ln2_b, L0_attn_att_tmk, L0_attn_att_tmv, L0_attn_att_tmr, L0_attn_time_decay, L0_attn_time_first, L0_attn_Wk, L0_attn_Wv, L0_attn_Wr, L0_attn_Wo, L0_attn_ffn_tmk, L0_attn_ffn_tmr, L0_attn_Wkey, L0_attn_Wrec, L0_attn_Wval, L0_ffn_w_gate, L0_ffn_w_up, L0_ffn_w_down):
    import jax
    import jax.numpy as jnp

    def _L0_tok_ref(x, W, b):
        import jax, jax.numpy as jnp
        import numpy as np
        IMG = 96
        P = 16
        C = 3
        D = 256
        B = 64
        Bsz, Cc, H, Wd = x.shape
        gh, gw = (H // P, Wd // P)
        patches = x.reshape(Bsz, Cc, gh, P, gw, P).transpose(0, 2, 4, 1, 3, 5)
        patches = patches.reshape(Bsz, gh * gw, Cc * P * P)
        return jnp.einsum('bnf,df->bnd', patches, W) + b

    def _L0_attn_ref(x, ln1_w, ln1_b, ln2_w, ln2_b, att_tmk, att_tmv, att_tmr, time_decay, time_first, Wk, Wv, Wr, Wo, ffn_tmk, ffn_tmr, Wkey, Wrec, Wval):
        import jax, jax.numpy as jnp
        import numpy as np
        import math
        B, T, C = (8, 512, 256)
        DIM_ATT, DIM_FFN = (256, 1024)
        N_LAYER, LAYER_ID = (12, 1)
        EPS = 1e-05

        def layer_norm(x, w, b):
            mu = jnp.mean(x, axis=-1, keepdims=True)
            var = jnp.mean(jnp.square(x - mu), axis=-1, keepdims=True)
            return (x - mu) * jax.lax.rsqrt(var + EPS) * w + b

        def time_shift(x):
            return jnp.pad(x, ((0, 0), (1, 0), (0, 0)))[:, :-1, :]

        def wkv(time_decay, time_first, k, v):
            w = -jnp.exp(time_decay)
            u = time_first

            def step(carry, kv_t):
                aa, bb, pp = carry
                kt, vt = kv_t
                ww = u + kt
                qq = jnp.maximum(pp, ww)
                e1 = jnp.exp(pp - qq)
                e2 = jnp.exp(ww - qq)
                y = (e1 * aa + e2 * vt) / (e1 * bb + e2)
                ww2 = pp + w
                qq2 = jnp.maximum(ww2, kt)
                e1b = jnp.exp(ww2 - qq2)
                e2b = jnp.exp(kt - qq2)
                return ((e1b * aa + e2b * vt, e1b * bb + e2b, qq2), y)
            init = (jnp.zeros_like(k[:, 0]), jnp.zeros_like(k[:, 0]), jnp.full_like(k[:, 0], -1e+38))
            kT = jnp.swapaxes(k, 0, 1)
            vT = jnp.swapaxes(v, 0, 1)
            _, yT = jax.lax.scan(step, init, (kT, vT))
            return jnp.swapaxes(yT, 0, 1)
        h = layer_norm(x, ln1_w, ln1_b)
        hh = time_shift(h)
        xk = h * att_tmk + hh * (1 - att_tmk)
        xv = h * att_tmv + hh * (1 - att_tmv)
        xr = h * att_tmr + hh * (1 - att_tmr)
        k = xk @ Wk.T
        v = xv @ Wv.T
        sr = jax.nn.sigmoid(xr @ Wr.T)
        rwkv = sr * wkv(time_decay, time_first, k, v)
        x = x + rwkv @ Wo.T
        h = layer_norm(x, ln2_w, ln2_b)
        hh = time_shift(h)
        xk = h * ffn_tmk + hh * (1 - ffn_tmk)
        xr = h * ffn_tmr + hh * (1 - ffn_tmr)
        kk = jnp.square(jax.nn.relu(xk @ Wkey.T))
        kv = kk @ Wval.T
        x = x + jax.nn.sigmoid(xr @ Wrec.T) * kv
        return x

    def _L0_ffn_ref(x, w_gate, w_up, w_down):
        import jax, jax.numpy as jnp
        import numpy as np
        BLOCK = 32
        W_BITS = 4
        ACT_BITS = 16

        def act_qdq(x):
            qmax = 2.0 ** (ACT_BITS - 1) - 1.0
            scale = jnp.maximum(jnp.max(jnp.abs(x)) / qmax, 1e-12)
            return jnp.clip(jnp.round(x / scale), -qmax - 1.0, qmax) * scale

        def fixed_qdq_u16(x):
            scale = 1.0 / 65536.0
            return jnp.clip(jnp.round(x / scale), 0.0, 65535.0) * scale

        def lpbq_dequant(w):
            O, I = w.shape
            qmax = 2.0 ** (W_BITS - 1) - 1.0
            wb = w.reshape(O, I // BLOCK, BLOCK)
            s = jnp.maximum(jnp.max(jnp.abs(wb), axis=-1, keepdims=True) / qmax, 1e-12)
            wq = jnp.clip(jnp.round(wb / s), -qmax - 1.0, qmax) * s
            return wq.reshape(O, I)
        x = act_qdq(x)
        up = act_qdq(x @ lpbq_dequant(w_up).T)
        gate = act_qdq(x @ lpbq_dequant(w_gate).T)
        sig = fixed_qdq_u16(jax.nn.sigmoid(gate))
        gate = act_qdq(gate * sig)
        o = act_qdq(gate * up)
        return o @ lpbq_dequant(w_down).T
    h = _L0_tok_ref(x, L0_tok_W, L0_tok_b)
    h = h + _L0_attn_ref(_layernorm(h, axis=-1), L0_attn_ln1_w, L0_attn_ln1_b, L0_attn_ln2_w, L0_attn_ln2_b, L0_attn_att_tmk, L0_attn_att_tmv, L0_attn_att_tmr, L0_attn_time_decay, L0_attn_time_first, L0_attn_Wk, L0_attn_Wv, L0_attn_Wr, L0_attn_Wo, L0_attn_ffn_tmk, L0_attn_ffn_tmr, L0_attn_Wkey, L0_attn_Wrec, L0_attn_Wval)
    h = h + _L0_ffn_ref(_layernorm(h, axis=-1), L0_ffn_w_gate, L0_ffn_w_up, L0_ffn_w_down)
    return h

_drawn_inputs = setup_inputs


def setup_inputs(seed=0):
    import zlib

    import numpy as np

    out = dict(_drawn_inputs(seed))
    spreads = {'L0_attn_ln1_w': (1.0, 0.2),
     'L0_attn_ln1_b': (0.0, 0.1),
     'L0_attn_ln2_w': (1.0, 0.2),
     'L0_attn_ln2_b': (0.0, 0.1)}
    factors = {'L0_ffn_w_gate': 3.214, 'L0_ffn_w_up': 3.181, 'L0_ffn_w_down': 3.193}
    for name, (base, spread) in spreads.items():
        noise = np.random.default_rng([zlib.crc32(name.encode()), seed]).standard_normal(out[name].shape)
        drawn = base * np.exp(spread * noise) if base else spread * noise
        out[name] = jnp.asarray(drawn.astype(out[name].dtype))
    for name, factor in factors.items():
        out[name] = (out[name] * factor).astype(out[name].dtype)
    return out
```

```python
import concourse.bass as bass
from concourse import mybir
from contextlib import ExitStack

P = 128
D = 256
FB = D // P
IMGS, TOK = 16, 36
NT = IMGS * TOK
PATCH = 3 * 16 * 16
PK = PATCH // P
CH = 2
CI = IMGS // CH
CT = NT // CH
TP = TOK + 1
PW = CI * TP
HK = 1024 // P
FF = 768
FK = FF // P
QB = 32
NQB = FF * D // P // QB
LN_EPS = 1e-5
NEG = -1e38
RND = 1.5 * 2.0 ** 23
QMAX = 32767.0
TINY = 1e-12

VECS = ["L0_tok_b", "L0_attn_ln1_w", "L0_attn_ln1_b", "L0_attn_ln2_w", "L0_attn_ln2_b", "L0_attn_att_tmk",
        "L0_attn_att_tmv", "L0_attn_att_tmr", "L0_attn_time_decay", "L0_attn_time_first", "L0_attn_ffn_tmk",
        "L0_attn_ffn_tmr"]


def build(nc, patches_d, vecs_d, wtok_d, wk_d, wv_d, wr_d, wo_d, wrec_d, wkey_d, wval_d, wgate_d, wup_d,
          wdown_d, out_d):
    fp32 = mybir.dt.float32
    ALU = mybir.AluOpType
    ACT = mybir.ActivationFunctionType
    AX = mybir.AxisListType

    ctx = ExitStack()
    with ctx:
        def sb(name, *shape):
            return ctx.enter_context(nc.sbuf_tensor(name, list(shape), fp32))

        def sem(name):
            return ctx.enter_context(nc.semaphore(name))

        patches = sb("patches", P, CH, PK, CT)
        vecs = sb("vecs", P, len(VECS), FB)
        wtok = sb("wtok", P, PK, D)
        wk, wv, wr, wo, wrec = (sb(n, P, FB, D) for n in ("wk", "wv", "wr", "wo", "wrec"))
        wkey = sb("wkey", P, FB, HK * P)
        wval = sb("wval", P, HK, D)
        ffn_raw = sb("ffn_raw", P, 3, FF * D // P)
        ffn_w = sb("ffn_w", P, 3, FF * D // P)
        wgate = ffn_w[:, 0, :].rearrange("p (k n) -> p k n", k=FB)
        wup = ffn_w[:, 1, :].rearrange("p (k n) -> p k n", k=FB)
        wdown = ffn_w[:, 2, :].rearrange("p (k n) -> p k n", k=FK)
        tok_b, ln1_w, ln1_b, ln2_w, ln2_b, tmk, tmv, tmr, decay, first, ftmk, ftmr = (
            vecs[:, i, :] for i in range(len(VECS)))

        ident = sb("ident", P, P)
        mean_w = sb("mean_w", P, P)
        ones_row = sb("ones_row", 1, P)
        eps1 = sb("eps1", P, 1)
        eps2 = sb("eps2", P, 1)
        rnd = sb("rnd", P, 1)
        wneg = sb("wneg", P, FB)
        wseg = sb("wseg", P, FB, CI, TP)
        bmax = sb("bmax", P, 3, NQB)
        binv = sb("binv", P, 3, NQB)

        h = sb("h", P, FB, NT)
        dev = sb("dev", P, FB, NT)
        sq = sb("sq", P, FB, NT)
        lnr = sb("lnr", P, CH, 2, CT)
        x0 = sb("x0", P, FB, NT)
        hn = sb("hn", P, FB, IMGS, TP)
        dm = sb("dm", P, FB, NT)
        xk, xv, xr = (sb(n, P, FB, NT) for n in ("xk", "xv", "xr"))
        hidden = ffn_raw[:, :, :].rearrange("p a b -> p (a b)").rearrange("p (k t) -> p k t", t=NT)
        PT = FB * IMGS * TP
        arena = sb("arena", P, 12 * PT)

        def padded(i, n=1):
            return arena[:, i * PT:(i + n) * PT].rearrange("p (b i t) -> p b i t", i=IMGS, t=TP)

        kp = padded(0)
        pp = padded(1)
        ex = [padded(2 + j) for j in range(4)]
        ex01, ex23 = padded(2, 2), padded(4, 2)
        ev = padded(6)
        aa, bb = padded(7), padded(8)

        def plain(i):
            return arena[:, i * PT:i * PT + FB * NT].rearrange("p (b t) -> p b t", t=NT)

        v = plain(9)
        z = plain(10)
        ea = plain(11)
        num, den = sq, dm
        tmp = sb("tmp", P, FB, NT)

        def big(i):
            return arena[:, i * FK * NT:(i + 1) * FK * NT].rearrange("p (k t) -> p k t", t=NT)

        gate, up, sig = big(0), big(1), big(2)
        mx = sb("mx", P, 5, FK)
        mx1 = sb("mx1", P, 5)
        top = sb("top", 1, 5)
        sc = sb("sc", P, 5)
        isc = sb("isc", P, 5)
        fac = sb("fac", P, 5)
        raw = sb("raw", P, 5)
        ps = ctx.enter_context(nc.psum_tensor("ps", [P, 8, 512], fp32))

        names = (["in_patch%d" % c for c in range(CH)] + ["in_" + n for n in (
            "vecs", "wtok", "wk", "wv", "wr", "wo", "wrec", "wkey", "wval", "ffn0", "ffn1", "ffn2")] + ["stored"])
        dma = {n: sem(n) for n in names}
        zeroed, const_ready, ident_ready = sem("zeroed"), sem("const_ready"), sem("ident_ready")
        wneg_ready, wseg_ready = sem("wneg_ready"), sem("wseg_ready")
        bmax_ready, bscale_ready, binv_ready = sem("bmax_ready"), sem("bscale_ready"), sem("binv_ready")
        wdiv_ready, wround_ready, wq_ready = sem("wdiv_ready"), sem("wround_ready"), sem("wq_ready")
        wt_done, wt_ready = sem("wt_done"), sem("wt_ready")
        (tok_done, mean_done, var_done, k_done, v_done, r_done, o_done, rec_done, key_done, val_done) = (
            sem(n) for n in ("tok_done", "mean_done", "var_done", "k_done", "v_done", "r_done", "o_done",
                             "rec_done", "key_done", "val_done"))
        gate_done, up_done, down_done = sem("gate_done"), sem("up_done"), sem("down_done")
        h_ready, dev_ready, sq_ready, ln_ready, rstd_ready = (
            sem(n) for n in ("h_ready", "dev_ready", "sq_ready", "ln_ready", "rstd_ready"))
        norm_ready, x0_ready, hn_ready, dm_ready, mix_ready = (
            sem(n) for n in ("norm_ready", "x0_ready", "hn_ready", "dm_ready", "mix_ready"))
        kp_ready, v_ready, z_ready, abs_ready, ea_ready = (
            sem(n) for n in ("kp_ready", "v_ready", "z_ready", "abs_ready", "ea_ready"))
        pp_ready, arg01_ready, arg23_ready, diff_ready, exp01_ready, exp23_ready = (
            sem(n) for n in ("pp_ready", "arg01_ready", "arg23_ready", "diff_ready", "exp01_ready", "exp23_ready"))
        ev_ready, state_ready, n2_ready, part_ready, frac_ready = (
            sem(n) for n in ("ev_ready", "state_ready", "n2_ready", "part_ready", "frac_ready"))
        scaled_ready, lnden_ready, logq_ready, quot_ready, rw_ready = (
            sem(n) for n in ("scaled_ready", "lnden_ready", "logq_ready", "quot_ready", "rw_ready"))
        x1_ready, hx_ready, relu_ready, hid_ready = (
            sem(n) for n in ("x1_ready", "hx_ready", "relu_ready", "hid_ready"))
        soft_ready, logsig_ready, recsig_ready, gated_ready, h2_ready = (
            sem(n) for n in ("soft_ready", "logsig_ready", "recsig_ready", "gated_ready", "h2_ready"))
        mx_ready, mx1_ready, mxt_done, top_ready, topb_done, scale_step, scale_ready = (
            sem(n) for n in ("mx_ready", "mx1_ready", "mxt_done", "top_ready", "topb_done", "scale_step",
                             "scale_ready"))
        mxsilu_ready = sem("mxsilu_ready")
        xbig_ready, xq_ready = sem("xbig_ready"), sem("xq_ready")
        gate_ready, up_ready = sem("gate_ready"), sem("up_ready")
        gbig_ready, gq_ready, sig_ready, clip_ready, sbig_ready, silu_ready = (
            sem(n) for n in ("gbig_ready", "gq_ready", "sig_ready", "clip_ready", "sbig_ready", "silu_ready"))
        tbig_ready, ubig_ready, uq_ready, prod_ready, obig_ready, oq_ready, out_ready = (
            sem(n) for n in ("tbig_ready", "ubig_ready", "uq_ready", "prod_ready", "obig_ready", "oq_ready",
                             "out_ready"))

        def cols(t, c):
            return t[:, :, c * CT:(c + 1) * CT]

        def imgs(t, c, b=None):
            t = cols(t, c) if b is None else t[:, b, c * CT:(c + 1) * CT]
            return t.rearrange("p b (i t) -> p b i t" if b is None else "p (i t) -> p i t", t=TOK)

        def now(t, c, b=None):
            s = slice(c * CI, (c + 1) * CI)
            return t[:, :, s, 1:TP] if b is None else t[:, b, s, 1:TP]

        def before(t, c, b=None):
            s = slice(c * CI, (c + 1) * CI)
            return t[:, :, s, 0:TOK] if b is None else t[:, b, s, 0:TOK]

        def run(t, c, b):
            return t[:, b, c * CI:(c + 1) * CI, :].rearrange("p i t -> p (i t)")

        def bank(n, count=1):
            return ps[:, n, 0:CT] if count == 1 else ps[:, n:n + count, 0:CT]

        def bank_imgs(n):
            return ps[:, n:n + 2, 0:CT].rearrange("p b (i t) -> p b i t", t=TOK)

        def twice(ap):
            return ap.unsqueeze(1).to_broadcast([P, FB, CT])

        TOKB, MEAN1, VAR1 = (0, 2), (4, 5), (6, 7)
        KB, VB, RB = (0, 6), (2, 0), (4, 2)
        WTB = (4, 5)
        OB, MEAN2, VAR2, RECB, KEYB, VALB = (6, 0), (2, 0), (3, 1), (4, 0), (2, 3), (6, 4)
        MEAN3, VAR3 = (6, 2), (7, 3)
        MEAN, VAR = (MEAN1, MEAN2, MEAN3), (VAR1, VAR2, VAR3)
        MXT, TOPB = 6, 7
        block = ctx.enter_context(nc.Block())

        @block.sync
        def _(sp):
            sp.dma_start(wtok[:, :, :], wtok_d).then_inc(dma["in_wtok"], 16)
            for c in range(CH):
                sp.dma_start(patches[:, c, :, :], patches_d[:, c, :, :]).then_inc(dma["in_patch%d" % c], 16)
            sp.dma_start(wk[:, :, :], wk_d).then_inc(dma["in_wk"], 16)
            sp.dma_start(wv[:, :, :], wv_d).then_inc(dma["in_wv"], 16)
            sp.dma_start(wr[:, :, :], wr_d).then_inc(dma["in_wr"], 16)
            for i, w in enumerate((wgate_d, wup_d, wdown_d)):
                sp.dma_start(ffn_raw[:, i, :], w).then_inc(dma["in_ffn%d" % i], 16)
            sp.dma_start(wo[:, :, :], wo_d).then_inc(dma["in_wo"], 16)
            sp.dma_start(wrec[:, :, :], wrec_d).then_inc(dma["in_wrec"], 16)
            sp.dma_start(wkey[:, :, :], wkey_d).then_inc(dma["in_wkey"], 16)
            sp.dma_start(wval[:, :, :], wval_d).then_inc(dma["in_wval"], 16)
            for c in range(CH):
                for m in range(FB):
                    sp.wait_ge(out_ready, FB * c + m + 1)
                    sp.dma_start(out_d[:, m, c * CT:(c + 1) * CT], x0[:, m, c * CT:(c + 1) * CT])\
                        .then_inc(dma["stored"], 16)
            sp.wait_ge(dma["stored"], 16 * CH * FB)

        @block.gpsimd
        def _(pool):
            pool.memset(ident[:, :], 0.0).then_inc(zeroed, 1)
            pool.memset(mean_w[:, :], 1.0 / D).then_inc(const_ready, 1)
            pool.memset(ones_row[:, :], 1.0).then_inc(const_ready, 1)
            pool.memset(eps1[:, :], LN_EPS).then_inc(const_ready, 1)
            pool.memset(eps2[:, :], LN_EPS * LN_EPS).then_inc(const_ready, 1)
            pool.memset(rnd[:, :], RND).then_inc(const_ready, 1)
            pool.wait_ge(zeroed, 1)
            pool.affine_select(out=ident[:, :], in_=ident[:, :], compare_op=ALU.not_equal, fill=1.0, base=0,
                               pattern=[[-1, P]], channel_multiplier=1).then_inc(ident_ready, 1)
            pool.memset(hn[:, :, :, 0:1], 0.0).then_inc(const_ready, 1)
            pool.memset(kp[:, :, :, 0:1], NEG).then_inc(const_ready, 1)
            for j in (0, 1):
                pool.memset(ex[j][:, :, :, 0:1], 0.0).then_inc(const_ready, 1)
            pool.memset(ev[:, :, :, 0:1], 0.0).then_inc(const_ready, 1)
            pool.memset(wseg[:, :, :, 0:1], NEG).then_inc(const_ready, 1)
            def weights(i):
                w3 = ffn_raw[:, i, :].rearrange("p (n q) -> p n q", q=QB)
                pool.wait_ge(binv_ready, i + 1)
                pool.tensor_tensor(w3, w3, binv[:, i, :].unsqueeze(2).to_broadcast([P, NQB, QB]),
                                   ALU.mult).then_inc(wdiv_ready, 1)
                pool.wait_ge(wround_ready, i + 1)
                pool.tensor_tensor(w3, w3, bmax[:, i, :].unsqueeze(2).to_broadcast([P, NQB, QB]),
                                   ALU.mult).then_inc(wq_ready, 1)

            def bonus(c):
                pool.wait_ge(exp23_ready, c + 1)
                pool.wait_ge(v_ready, c + 1)
                pool.tensor_tensor(imgs(tmp, c), now(ex[3], c), imgs(v, c), ALU.mult).then_inc(n2_ready, 1)

            weights(0)
            weights(1)
            bonus(0)
            weights(2)
            bonus(1)

            def hx(c):
                pool.wait_ge(x1_ready, c + 1)
                pool.tensor_tensor(cols(h, c), cols(h, c), cols(x0, c), ALU.add).then_inc(hx_ready, 1)

            def squares(c):
                for m in range(HK):
                    pool.wait_ge(relu_ready, HK * c + m + 1)
                    t = hidden[:, m, c * CT:(c + 1) * CT]
                    pool.tensor_tensor(t, t, t, ALU.mult).then_inc(hid_ready, 1)

            for c in range(CH):
                hx(c)
                squares(c)

        @block.scalar
        def _(act):
            act.dma_start(vecs[:, :, :], vecs_d).then_inc(dma["in_vecs"], 16)
            act.preload_act_table_set("natural_log_exp_and_others")
            act.wait_ge(dma["in_vecs"], 16)
            act.activation(wneg[:, :], decay, ACT.Exp).then_inc(wneg_ready, 1)
            act.wait_ge(const_ready, 5)

            def embed(c):
                act.wait_ge(tok_done, c + 1)
                for b in range(FB):
                    act.activation(h[:, b, c * CT:(c + 1) * CT], bank(TOKB[c] + b), ACT.Identity,
                                   bias=tok_b[:, b:b + 1]).then_inc(h_ready, 1)

            def square(n, c):
                act.wait_ge(dev_ready, CH * n + c + 1)
                act.activation(cols(sq, c), cols(dev, c), ACT.Square).then_inc(sq_ready, 1)

            def rstd(n, c):
                act.wait_ge(var_done, CH * n + c + 1)
                t = lnr[:, c, 0, :]
                act.activation(t, bank(VAR[n][c]), ACT.Ln, bias=eps1[:, :]).then_inc(ln_ready, 1)
                if n == 0:
                    act.activation(lnr[:, c, 1, :], bank(VAR[n][c]), ACT.Ln, bias=eps2[:, :],
                                   scale=1.0 + LN_EPS).then_inc(ln_ready, 1)
                    t = lnr[:, c, :, :]
                    act.wait_ge(ln_ready, 2 * (c + 1))
                else:
                    act.wait_ge(ln_ready, 2 * CH + CH * (n - 1) + c + 1)
                act.activation(t, t, ACT.Exp, scale=-0.5).then_inc(rstd_ready, 1)

            def affine(n, c):
                act.wait_ge(norm_ready, CH * n + c + 1)
                for b in range(FB):
                    w, o = ((ln1_w, ln1_b), (ln2_w, ln2_b))[n]
                    act.activation(now(hn, c, b), imgs(dev, c, b), ACT.Identity, bias=o[:, b:b + 1],
                                   scale=w[:, b:b + 1]).then_inc(hn_ready, 1)

            def heads(c):
                act.wait_ge(k_done, c + 1)
                act.activation(now(kp, c), bank_imgs(KB[c]), ACT.Copy).then_inc(kp_ready, 1)
                act.wait_ge(v_done, c + 1)
                act.activation(cols(v, c), bank(VB[c], 2), ACT.Copy).then_inc(v_ready, 1)
                act.wait_ge(r_done, c + 1)
                act.activation(cols(z, c), bank(RB[c], 2), ACT.Copy).then_inc(z_ready, 1)
                act.activation(cols(ea, c), bank(RB[c], 2), ACT.Abs).then_inc(abs_ready, 1)
                act.wait_ge(abs_ready, c + 1)
                act.activation(cols(ea, c), cols(ea, c), ACT.Exp, scale=-1.0).then_inc(ea_ready, 1)

            def exps(c):
                for t, asked, done in ((ex01, arg01_ready, exp01_ready), (ex23, arg23_ready, exp23_ready)):
                    act.wait_ge(asked, c + 1)
                    act.activation(now(t, c), now(t, c), ACT.Exp).then_inc(done, 1)

            def lnden(c):
                act.wait_ge(scaled_ready, c + 1)
                act.activation(cols(den, c), cols(den, c), ACT.Ln).then_inc(lnden_ready, 1)

            def quot(c):
                act.wait_ge(logq_ready, c + 1)
                act.activation(cols(den, c), cols(den, c), ACT.Exp).then_inc(quot_ready, 1)

            def weights_out(g0, g1):
                flat = ffn_w[:, :, :].rearrange("p a b -> p (a b)")
                for g in range(g0, g1):
                    act.wait_ge(wt_done, g + 1)
                    act.activation(flat[:, g * 512:(g + 1) * 512], ps[:, WTB[g % 2], :], ACT.Copy)\
                        .then_inc(wt_ready, 1)

            def soft(c):
                act.wait_ge(rec_done, c + 1)
                act.wait_ge(logq_ready, c + 1)
                act.wait_ge(scaled_ready, c + 1)
                act.activation(cols(z, c), bank(RECB[c], 2), ACT.Copy).then_inc(z_ready, 1)
                act.activation(cols(ea, c), bank(RECB[c], 2), ACT.Abs).then_inc(abs_ready, 1)
                act.wait_ge(abs_ready, CH + c + 1)
                act.activation(cols(ea, c), cols(ea, c), ACT.Exp, scale=-1.0).then_inc(ea_ready, 1)
                act.wait_ge(ea_ready, CH + c + 1)
                act.activation(cols(ea, c), cols(ea, c), ACT.Ln, bias=1.0).then_inc(soft_ready, 1)

            def recsig(c):
                act.wait_ge(logsig_ready, c + 1)
                act.activation(cols(ea, c), cols(ea, c), ACT.Exp).then_inc(recsig_ready, 1)

            def relu(c, m):
                act.wait_ge(key_done, HK * c + m + 1)
                if c == 0 and m == 0:
                    act.wait_ge(wt_done, 9)
                act.activation(hidden[:, m, c * CT:(c + 1) * CT], bank(KEYB[m % 2]), ACT.Relu)\
                    .then_inc(relu_ready, 1)

            embed(0)
            embed(1)
            square(0, 0)
            square(0, 1)
            rstd(0, 0)
            rstd(0, 1)
            affine(0, 0)
            affine(0, 1)
            heads(0)
            exps(0)
            heads(1)
            exps(1)
            weights_out(0, 3)
            lnden(0)
            quot(0)
            weights_out(3, 9)
            square(1, 0)
            rstd(1, 0)
            lnden(1)
            quot(1)
            affine(1, 0)
            soft(0)
            recsig(0)
            for m in range(HK):
                relu(0, m)
            square(1, 1)
            rstd(1, 1)
            affine(1, 1)
            soft(1)
            recsig(1)
            for m in range(4):
                relu(1, m)
            square(2, 0)
            rstd(2, 0)
            for m in range(4, HK):
                relu(1, m)
            square(2, 1)
            rstd(2, 1)
            act.preload_act_table_set("sigmoid_and_others")

            act.wait_ge(scale_ready, 1)
            for c in range(CH):
                act.activation(cols(xk, c), cols(dev, c), ACT.Identity, bias=rnd[:, :], scale=fac[:, 0:1])\
                    .then_inc(xbig_ready, 1)

            def evacuate(dst, done, ready, m):
                for c in range(CH):
                    act.wait_ge(done, CH * m + c + 1)
                    act.activation(dst[:, m, c * CT:(c + 1) * CT], bank((CH * m + c) % 6), ACT.Copy)\
                        .then_inc(ready, 1)

            for m in range(FK):
                evacuate(gate, gate_done, gate_ready, m)
            act.wait_ge(scale_ready, 2)
            for m in range(FK):
                act.activation(gate[:, m, :], gate[:, m, :], ACT.Identity, bias=rnd[:, :], scale=fac[:, 1:2])\
                    .then_inc(gbig_ready, 1)
                evacuate(up, up_done, up_ready, m)
                if m >= 1:
                    act.wait_ge(gq_ready, m)
                    act.activation(sig[:, m - 1, :], gate[:, m - 1, :], ACT.Sigmoid, scale=sc[:, 1:2])\
                        .then_inc(sig_ready, 1)
            act.wait_ge(gq_ready, FK)
            act.activation(sig[:, FK - 1, :], gate[:, FK - 1, :], ACT.Sigmoid, scale=sc[:, 1:2])\
                .then_inc(sig_ready, 1)
            act.wait_ge(scale_ready, 3)
            for m in range(FK):
                act.activation(up[:, m, :], up[:, m, :], ACT.Identity, bias=rnd[:, :], scale=fac[:, 2:3])\
                    .then_inc(ubig_ready, 1)
            act.wait_ge(scale_ready, 4)
            for m in range(FK):
                act.activation(sig[:, m, :], sig[:, m, :], ACT.Identity, bias=rnd[:, :], scale=fac[:, 3:4])\
                    .then_inc(tbig_ready, 1)
            act.wait_ge(scale_ready, 5)
            for m in range(FK):
                act.activation(up[:, m, :], up[:, m, :], ACT.Identity, bias=rnd[:, :], scale=fac[:, 4:5])\
                    .then_inc(obig_ready, 1)

        @block.vector
        def _(dve):
            def round_weights(i):
                dve.wait_ge(dma["in_ffn%d" % i], 16)
                w3 = ffn_raw[:, i, :].rearrange("p (n q) -> p n q", q=QB)
                dve.tensor_reduce(bmax[:, i, :], w3, AX.X, ALU.max, apply_absolute_value=True)\
                    .then_inc(bmax_ready, 1)
                dve.wait_ge(bmax_ready, i + 1)
                dve.tensor_scalar(bmax[:, i, :], bmax[:, i, :], 1.0 / 7.0, TINY, ALU.mult, ALU.max)\
                    .then_inc(bscale_ready, 1)
                dve.wait_ge(bscale_ready, i + 1)
                dve.reciprocal(binv[:, i, :], bmax[:, i, :]).then_inc(binv_ready, 1)

            def round_weights2(i):
                dve.wait_ge(wdiv_ready, i + 1)
                dve.tensor_scalar(ffn_raw[:, i, :], ffn_raw[:, i, :], RND, RND, ALU.add, ALU.subtract)\
                    .then_inc(wround_ready, 1)

            def deviation(n, c):
                src = x0 if n == 1 else h
                dve.wait_ge(mean_done, CH * n + c + 1)
                dve.tensor_tensor(cols(dev, c), cols(src, c), twice(bank(MEAN[n][c])), ALU.subtract)\
                    .then_inc(dev_ready, 1)

            def normalise(n, c):
                dve.wait_ge(rstd_ready, CH * n + c + 1)
                if n == 0:
                    dve.tensor_tensor(cols(x0, c), cols(dev, c), twice(lnr[:, c, 0, :]), ALU.mult)\
                        .then_inc(x0_ready, 1)
                    dve.wait_ge(x0_ready, c + 1)
                dve.tensor_tensor(cols(dev, c), cols(dev, c), twice(lnr[:, c, 1 if n == 0 else 0, :]), ALU.mult)\
                    .then_inc(norm_ready, 1)

            def mix(n, c):
                dve.wait_ge(hn_ready, FB * (CH * n + c + 1))
                if n == 1:
                    dve.wait_ge(rw_ready, c + 1)
                dve.tensor_tensor(imgs(dm, c), now(hn, c), before(hn, c), ALU.subtract).then_inc(dm_ready, 1)
                dve.wait_ge(dm_ready, CH * n + c + 1)
                pairs = ((xk, tmk), (xv, tmv), (xr, tmr)) if n == 0 else ((xk, ftmk), (xr, ftmr))
                for dst, m in pairs:
                    for b in range(FB):
                        dve.scalar_tensor_tensor(imgs(dst, c, b), imgs(dm, c, b), m[:, b:b + 1],
                                                 before(hn, c, b), ALU.mult, ALU.add).then_inc(mix_ready, 1)

            def maxima(c):
                dve.wait_ge(kp_ready, c + 1)
                for b in range(FB):
                    dve.tensor_tensor_scan(run(pp, c, b), wseg[:, b, :, :].rearrange("p i t -> p (i t)"),
                                           run(kp, c, b), NEG, ALU.add, ALU.max).then_inc(pp_ready, 1)
                dve.wait_ge(pp_ready, FB * (c + 1))
                for b in range(FB):
                    dve.scalar_tensor_tensor(now(ex[0], c, b), before(pp, c, b), wneg[:, b:b + 1],
                                             now(pp, c, b), ALU.add, ALU.subtract)
                dve.tensor_tensor(now(ex[1], c), now(kp, c), now(pp, c), ALU.subtract).then_inc(arg01_ready, 1)
                for b in range(FB):
                    dve.scalar_tensor_tensor(now(ex[3], c, b), now(kp, c, b), first[:, b:b + 1],
                                             before(pp, c, b), ALU.add, ALU.subtract).then_inc(diff_ready, 1)
                dve.wait_ge(diff_ready, FB * (c + 1) + c)
                dve.tensor_scalar(now(ex[2], c), now(ex[3], c), 0.0, -1.0, ALU.max, ALU.mult)\
                    .then_inc(diff_ready, 1)
                dve.wait_ge(diff_ready, (FB + 1) * (c + 1))
                dve.tensor_scalar(now(ex[3], c), now(ex[3], c), 0.0, None, ALU.min).then_inc(arg23_ready, 1)

            def states(c):
                dve.wait_ge(exp01_ready, c + 1)
                dve.wait_ge(v_ready, c + 1)
                dve.tensor_tensor(now(ev, c), now(ex[1], c), imgs(v, c), ALU.mult).then_inc(ev_ready, 1)
                for b in range(FB):
                    dve.tensor_tensor_scan(run(bb, c, b), run(ex[0], c, b), run(ex[1], c, b), 0.0,
                                           ALU.mult, ALU.add).then_inc(state_ready, 1)
                dve.wait_ge(ev_ready, c + 1)
                for b in range(FB):
                    dve.tensor_tensor_scan(run(aa, c, b), run(ex[0], c, b), run(ev, c, b), 0.0,
                                           ALU.mult, ALU.add).then_inc(state_ready, 1)

            def fraction(c):
                dve.wait_ge(exp23_ready, c + 1)
                dve.wait_ge(state_ready, 2 * FB * (c + 1))
                dve.tensor_tensor(imgs(den, c), now(ex[2], c), before(bb, c), ALU.mult).then_inc(part_ready, 1)
                dve.tensor_tensor(imgs(num, c), now(ex[2], c), before(aa, c), ALU.mult).then_inc(part_ready, 1)
                dve.wait_ge(part_ready, 2 * c + 1)
                dve.tensor_tensor(imgs(den, c), imgs(den, c), now(ex[3], c), ALU.add).then_inc(frac_ready, 1)
                dve.wait_ge(n2_ready, c + 1)
                dve.wait_ge(part_ready, 2 * c + 2)
                dve.tensor_tensor(cols(num, c), cols(num, c), cols(tmp, c), ALU.add).then_inc(frac_ready, 1)
                dve.wait_ge(frac_ready, 2 * c + 1)
                dve.wait_ge(ea_ready, c + 1)
                dve.scalar_tensor_tensor(cols(den, c), cols(ea, c), 1.0, cols(den, c), ALU.add, ALU.mult)\
                    .then_inc(scaled_ready, 1)

            def logq(c):
                dve.wait_ge(lnden_ready, c + 1)
                dve.scalar_tensor_tensor(cols(den, c), cols(z, c), 0.0, cols(den, c), ALU.min, ALU.subtract)\
                    .then_inc(logq_ready, 1)

            def rwkv(c):
                dve.wait_ge(quot_ready, c + 1)
                dve.wait_ge(frac_ready, 2 * c + 2)
                dve.tensor_tensor(cols(xk, c), cols(num, c), cols(den, c), ALU.mult).then_inc(rw_ready, 1)

            def residual(c):
                dve.wait_ge(o_done, c + 1)
                dve.tensor_tensor(cols(x0, c), cols(x0, c), bank(OB[c], 2), ALU.add).then_inc(x1_ready, 1)

            def logsig(c):
                dve.wait_ge(soft_ready, c + 1)
                dve.scalar_tensor_tensor(cols(ea, c), cols(z, c), 0.0, cols(ea, c), ALU.min, ALU.subtract)\
                    .then_inc(logsig_ready, 1)

            def channel_out(c):
                dve.wait_ge(val_done, c + 1)
                dve.wait_ge(recsig_ready, c + 1)
                dve.tensor_tensor(cols(xv, c), cols(ea, c), bank(VALB[c], 2), ALU.mult).then_inc(gated_ready, 1)
                dve.wait_ge(gated_ready, c + 1)
                dve.wait_ge(hx_ready, c + 1)
                dve.tensor_tensor(cols(h, c), cols(h, c), cols(xv, c), ALU.add).then_inc(h2_ready, 1)

            dve.wait_ge(wneg_ready, 1)
            dve.tensor_scalar(wneg[:, :], wneg[:, :], -1.0, None, ALU.mult).then_inc(wneg_ready, 1)
            dve.wait_ge(wneg_ready, 2)
            dve.memset(wseg[:, :, :, 1:TP], 0.0).then_inc(wseg_ready, 1)
            dve.wait_ge(wseg_ready, 1)
            for b in range(FB):
                dve.tensor_scalar(wseg[:, b, :, 1:TP], wseg[:, b, :, 1:TP], wneg[:, b:b + 1], None, ALU.add)\
                    .then_inc(wseg_ready, 1)
            dve.wait_ge(wseg_ready, 1 + FB)
            deviation(0, 0)
            deviation(0, 1)
            round_weights(0)
            normalise(0, 0)
            normalise(0, 1)
            dve.wait_ge(const_ready, 11)
            mix(0, 0)
            mix(0, 1)
            round_weights2(0)
            round_weights(1)
            maxima(0)
            round_weights2(1)
            round_weights(2)
            states(0)
            maxima(1)
            fraction(0)
            round_weights2(2)
            logq(0)
            rwkv(0)
            states(1)
            residual(0)
            deviation(1, 0)
            fraction(1)
            logq(1)
            normalise(1, 0)
            rwkv(1)
            mix(1, 0)
            logsig(0)
            residual(1)
            deviation(1, 1)
            normalise(1, 1)
            mix(1, 1)
            logsig(1)
            channel_out(0)
            deviation(2, 0)
            normalise(2, 0)
            dve.wait_ge(norm_ready, 2 * CH + 1)
            dve.tensor_reduce(mx[:, 0, 0:1], cols(dev, 0), AX.XY, ALU.max, apply_absolute_value=True)\
                .then_inc(mx_ready, 1)
            channel_out(1)
            deviation(2, 1)
            normalise(2, 1)
            dve.wait_ge(norm_ready, 2 * CH + 2)
            dve.tensor_reduce(mx[:, 0, 1:2], cols(dev, 1), AX.XY, ALU.max, apply_absolute_value=True)\
                .then_inc(mx_ready, 1)

            def reduce_max(i, count, ready, seen):
                dve.wait_ge(ready, seen)
                dve.tensor_reduce(mx1[:, i:i + 1], mx[:, i, 0:count], AX.X, ALU.max).then_inc(mx1_ready, 1)

            def core_max(i):
                dve.wait_ge(mxt_done, i + 1)
                dve.tensor_reduce(top[0:1, i:i + 1], ps[0:1, MXT, 0:P], AX.X, ALU.max).then_inc(top_ready, 1)

            steps = [0]

            def small(ins):
                steps[0] += 1
                ins.then_inc(scale_step, 1)
                dve.wait_ge(scale_step, steps[0])

            def scale(i, one):
                dve.wait_ge(topb_done, i + 1)
                if one is None:
                    small(dve.tensor_scalar(sc[:, i:i + 1], ps[:, TOPB, 0:1], 1.0 / QMAX, TINY, ALU.mult, ALU.max))
                    dve.reciprocal(fac[:, i:i + 1], sc[:, i:i + 1]).then_inc(scale_ready, 1)
                    return
                small(dve.tensor_scalar(raw[:, i:i + 1], ps[:, TOPB, 0:1], one, 1.0 / QMAX, ALU.mult, ALU.mult))
                small(dve.tensor_scalar(sc[:, i:i + 1], raw[:, i:i + 1], TINY, None, ALU.max))
                small(dve.reciprocal(isc[:, i:i + 1], sc[:, i:i + 1]))
                dve.tensor_scalar(fac[:, i:i + 1], isc[:, i:i + 1], one, None, ALU.mult).then_inc(scale_ready, 1)

            reduce_max(0, CH, mx_ready, CH)
            core_max(0)
            scale(0, None)
            for c in range(CH):
                dve.wait_ge(xbig_ready, c + 1)
                dve.tensor_scalar(cols(xk, c), cols(xk, c), RND, None, ALU.subtract).then_inc(xq_ready, 1)
            for m in range(FK):
                dve.wait_ge(gate_ready, CH * (m + 1))
                dve.tensor_reduce(mx[:, 1, m:m + 1], gate[:, m, :], AX.X, ALU.max, apply_absolute_value=True)\
                    .then_inc(mx_ready, 1)
            reduce_max(1, FK, mx_ready, CH + FK)
            core_max(1)
            scale(1, sc[:, 0:1])
            for m in range(FK + 2):
                if m < FK:
                    dve.wait_ge(gbig_ready, m + 1)
                    dve.tensor_scalar(gate[:, m, :], gate[:, m, :], RND, None, ALU.subtract).then_inc(gq_ready, 1)
                    dve.wait_ge(up_ready, CH * (m + 1))
                    dve.tensor_reduce(mx[:, 2, m:m + 1], up[:, m, :], AX.X, ALU.max, apply_absolute_value=True)\
                        .then_inc(mx_ready, 1)
                if m == FK - 1:
                    reduce_max(2, FK, mx_ready, CH + 2 * FK)
                if m == FK:
                    core_max(2)
                    scale(2, sc[:, 0:1])
                j = m - 2
                if j >= 0:
                    dve.wait_ge(sig_ready, j + 1)
                    dve.tensor_scalar(sig[:, j, :], sig[:, j, :], 65536.0, 65535.0, ALU.mult, ALU.min)\
                        .then_inc(clip_ready, 1)
                    dve.wait_ge(clip_ready, j + 1)
                    dve.tensor_scalar(sig[:, j, :], sig[:, j, :], RND, None, ALU.add).then_inc(sbig_ready, 1)
                    dve.wait_ge(sbig_ready, j + 1)
                    dve.scalar_tensor_tensor(sig[:, j, :], sig[:, j, :], RND, gate[:, j, :], ALU.subtract,
                                             ALU.mult).then_inc(silu_ready, 1)
                    dve.wait_ge(silu_ready, j + 1)
                    dve.tensor_reduce(mx[:, 3, j:j + 1], sig[:, j, :], AX.X, ALU.max, apply_absolute_value=True)\
                        .then_inc(mxsilu_ready, 1)
            reduce_max(3, FK, mxsilu_ready, FK)
            core_max(3)
            small(dve.tensor_scalar(raw[:, 0:1], sc[:, 1:2], 1.0 / 65536.0, None, ALU.mult))
            scale(3, raw[:, 0:1])
            for m in range(FK):
                dve.wait_ge(ubig_ready, m + 1)
                dve.tensor_scalar(up[:, m, :], up[:, m, :], RND, None, ALU.subtract).then_inc(uq_ready, 1)
            for m in range(FK):
                dve.wait_ge(tbig_ready, m + 1)
                dve.wait_ge(uq_ready, m + 1)
                dve.scalar_tensor_tensor(up[:, m, :], sig[:, m, :], RND, up[:, m, :], ALU.subtract, ALU.mult)\
                    .then_inc(prod_ready, 1)
                dve.wait_ge(prod_ready, m + 1)
                dve.tensor_reduce(mx[:, 4, m:m + 1], up[:, m, :], AX.X, ALU.max, apply_absolute_value=True)\
                    .then_inc(mx_ready, 1)
            reduce_max(4, FK, mx_ready, CH + 3 * FK)
            core_max(4)
            small(dve.tensor_scalar(mx1[:, 0:1], sc[:, 2:3], sc[:, 3:4], None, ALU.mult))
            scale(4, mx1[:, 0:1])
            for m in range(FK):
                dve.wait_ge(obig_ready, m + 1)
                dve.tensor_scalar(up[:, m, :], up[:, m, :], RND, None, ALU.subtract).then_inc(oq_ready, 1)
            for c in range(CH):
                for m in range(FB):
                    dve.wait_ge(down_done, FB * c + m + 1)
                    s = slice(c * CT, (c + 1) * CT)
                    dve.scalar_tensor_tensor(x0[:, m, s], bank(FB * c + m), sc[:, 4:5], h[:, m, s], ALU.mult,
                                             ALU.add).then_inc(out_ready, 1)

        @block.tensor
        def _(pe):
            def product(dst, w, src, m, c, blocks, rhs=None):
                for k in range(blocks):
                    r = src[:, k, c * CT:(c + 1) * CT] if rhs is None else rhs(k)
                    last = pe.matmul(dst, w[:, k, m * P:(m + 1) * P], r, start=(k == 0), stop=(k == blocks - 1))
                return last

            def embed(c):
                pe.wait_ge(dma["in_patch%d" % c], 16)
                for m in range(FB):
                    last = product(bank(TOKB[c] + m), wtok, None, m, c, PK, lambda k: patches[:, c, k, :])
                last.then_inc(tok_done, 1)

            def spread(dst, src, c):
                for k in range(FB):
                    last = pe.matmul(dst, mean_w[:, :], src[:, k, c * CT:(c + 1) * CT], start=(k == 0),
                                     stop=(k == FB - 1))
                return last

            def project(w, src, banks, done, c):
                for m in range(FB):
                    last = product(bank(banks[c] + m), w, src, m, c, FB)
                last.then_inc(done, 1)

            def heads(c):
                pe.wait_ge(mix_ready, 3 * FB * (c + 1))
                if c == 0:
                    pe.wait_ge(dma["in_wk"], 16)
                    pe.wait_ge(dma["in_wv"], 16)
                    pe.wait_ge(dma["in_wr"], 16)
                    pe.wait_ge(h_ready, FB * CH)
                    pe.wait_ge(dev_ready, CH)
                else:
                    pe.wait_ge(ln_ready, 2 * CH)
                    pe.wait_ge(kp_ready, 1)
                project(wk, xk, KB, k_done, c)
                project(wv, xv, VB, v_done, c)
                if c == 1:
                    pe.wait_ge(v_ready, 1)
                project(wr, xr, RB, r_done, c)

            def weights(i):
                pe.wait_ge(wq_ready, i + 1)
                if i == 0:
                    pe.wait_ge(ident_ready, 1)
                    pe.wait_ge(z_ready, 1)
                    pe.wait_ge(abs_ready, 1)
                kb, mb = (FB, FK) if i < 2 else (FK, FB)
                for g in range(3):
                    n = 3 * i + g
                    if n >= 2:
                        pe.wait_ge(wt_ready, n - 1)
                    for j in range(4):
                        k, m = divmod(4 * g + j, mb)
                        last = pe.transpose(ps[:, WTB[n % 2], j * P:(j + 1) * P],
                                            ffn_raw[:, i, (m * kb + k) * P:(m * kb + k + 1) * P], ident[:, :])
                    last.then_inc(wt_done, 1)

            def wkv_out(c):
                if c == 0:
                    pe.wait_ge(dma["in_wo"], 16)
                pe.wait_ge(kp_ready, CH)
                pe.wait_ge(v_ready, CH)
                pe.wait_ge(rw_ready, c + 1)
                project(wo, xk, OB, o_done, c)

            pe.wait_ge(dma["in_wtok"], 16)
            for c in range(CH):
                embed(c)
            pe.wait_ge(const_ready, 1)
            for c in range(CH):
                pe.wait_ge(h_ready, FB * (c + 1))
                spread(bank(MEAN1[c]), h, c).then_inc(mean_done, 1)
            for c in range(CH):
                pe.wait_ge(sq_ready, c + 1)
                spread(bank(VAR1[c]), sq, c).then_inc(var_done, 1)
            heads(0)
            heads(1)
            weights(0)
            weights(1)

            def norm2(c):
                pe.wait_ge(x1_ready, c + 1)
                if c == 0:
                    pe.wait_ge(z_ready, CH)
                    pe.wait_ge(abs_ready, CH)
                spread(bank(MEAN2[c]), x0, c).then_inc(mean_done, 1)
                pe.wait_ge(sq_ready, CH + c + 1)
                spread(bank(VAR2[c]), sq, c).then_inc(var_done, 1)

            def receptance(c):
                if c == 0:
                    pe.wait_ge(dma["in_wrec"], 16)
                    pe.wait_ge(wt_ready, 9)
                else:
                    pe.wait_ge(dev_ready, CH + 2)
                    pe.wait_ge(ln_ready, 3 * CH)
                pe.wait_ge(mix_ready, 3 * FB * CH + 2 * FB * (c + 1))
                project(wrec, xr, RECB, rec_done, c)

            def keys(c, m0, m1):
                if (c, m0) == (0, 0):
                    pe.wait_ge(dma["in_wkey"], 16)
                    pe.wait_ge(dev_ready, CH + 1)
                    pe.wait_ge(ln_ready, 2 * CH + 1)
                for m in range(m0, m1):
                    n = HK * c + m
                    if n >= 2:
                        pe.wait_ge(relu_ready, n - 1)
                    product(bank(KEYB[m % 2]), wkey, xk, m, c, FB).then_inc(key_done, 1)

            def values(c):
                if c == 0:
                    pe.wait_ge(dma["in_wval"], 16)
                else:
                    pe.wait_ge(z_ready, CH + 1)
                    pe.wait_ge(abs_ready, CH + 1)
                for k in range(HK):
                    pe.wait_ge(hid_ready, HK * c + k + 1)
                    for m in range(FB):
                        last = pe.matmul(bank(VALB[c] + m), wval[:, k, m * P:(m + 1) * P],
                                         hidden[:, k, c * CT:(c + 1) * CT], start=(k == 0), stop=(k == HK - 1))
                last.then_inc(val_done, 1)

            def norm3(c):
                pe.wait_ge(h2_ready, c + 1)
                if c == 1:
                    pe.wait_ge(relu_ready, HK * CH)
                spread(bank(MEAN3[c]), h, c).then_inc(mean_done, 1)
                pe.wait_ge(sq_ready, 2 * CH + c + 1)
                spread(bank(VAR3[c]), sq, c).then_inc(var_done, 1)

            wkv_out(0)
            weights(2)
            norm2(0)
            receptance(0)
            keys(0, 0, HK)
            wkv_out(1)
            norm2(1)
            values(0)
            receptance(1)
            keys(1, 0, 4)
            norm3(0)
            keys(1, 4, HK)
            values(1)
            norm3(1)

            def spread_max(i):
                pe.wait_ge(mx1_ready, i + 1)
                if i == 0:
                    pe.wait_ge(dev_ready, 3 * CH)
                    pe.wait_ge(ln_ready, 4 * CH)
                    pe.wait_ge(const_ready, 2)
                else:
                    pe.wait_ge(scale_ready, i)
                pe.transpose(ps[0:1, MXT, 0:P], mx1[:, i:i + 1], ident[:, :]).then_inc(mxt_done, 1)
                pe.wait_ge(top_ready, i + 1)
                pe.matmul(ps[:, TOPB, 0:1], ones_row[0:1, :], top[0:1, i:i + 1], start=True, stop=True)\
                    .then_inc(topb_done, 1)

            def expand(w, done, ready, before_ready):
                for m in range(FK):
                    for c in range(CH):
                        n = CH * m + c
                        if n < 6 and before_ready is not None:
                            pe.wait_ge(before_ready, CH * FK - 6 + n + 1)
                        if n >= 6:
                            pe.wait_ge(ready, n - 5)
                        if m == 0 and w is wgate:
                            pe.wait_ge(xq_ready, c + 1)
                        product(bank(n % 6), w, xk, m, c, FB).then_inc(done, 1)

            spread_max(0)
            pe.wait_ge(wt_ready, 9)
            expand(wgate, gate_done, gate_ready, None)
            spread_max(1)
            expand(wup, up_done, up_ready, gate_ready)
            spread_max(2)
            spread_max(3)
            spread_max(4)
            pe.wait_ge(up_ready, CH * FK)
            for c in range(CH):
                for m in range(FB):
                    for k in range(FK):
                        pe.wait_ge(oq_ready, k + 1)
                        last = pe.matmul(bank(FB * c + m), wdown[:, k, m * P:(m + 1) * P],
                                         up[:, k, c * CT:(c + 1) * CT], start=(k == 0), stop=(k == FK - 1))
                    last.then_inc(down_done, 1)


def kernel(**inputs):
    import numpy as np
    import concourse.bacc as bacc
    from concourse.bass_utils import run_bass_kernel_spmd

    def inner(w):
        return w.reshape(-1, P, w.shape[1]).transpose(1, 0, 2)

    def outer(w):
        return w.reshape(-1, P, w.shape[1]).transpose(1, 0, 2).reshape(P, -1)

    g = {n: np.asarray(a) for n, a in inputs.items()}
    side = g["x"].shape[-1] // 16
    x = g["x"].reshape(IMGS, 3, side, 16, side, 16).transpose(1, 3, 5, 0, 2, 4)
    arrays = {
        "patches": x.reshape(PK, P, CH, CT).transpose(1, 2, 0, 3),
        "vecs": np.stack([g[n].reshape(FB, P) for n in VECS]).transpose(2, 0, 1),
        "wtok": inner(g["L0_tok_W"].T),
        "wk": inner(g["L0_attn_Wk"].T), "wv": inner(g["L0_attn_Wv"].T), "wr": inner(g["L0_attn_Wr"].T),
        "wo": inner(g["L0_attn_Wo"].T), "wrec": inner(g["L0_attn_Wrec"].T), "wkey": inner(g["L0_attn_Wkey"].T),
        "wval": inner(g["L0_attn_Wval"].T),
        "wgate": outer(g["L0_ffn_w_gate"]), "wup": outer(g["L0_ffn_w_up"]), "wdown": outer(g["L0_ffn_w_down"]),
    }
    nc = bacc.Bacc("TRN2", target_bir_lowering=False, num_devices=1)
    feeds, args = {}, []
    for name, a in arrays.items():
        feeds[name + "_dram"] = np.ascontiguousarray(a)
        args.append(nc.dram_tensor(name + "_dram", a.shape, mybir.dt.float32, kind="ExternalInput").ap())
    out = nc.dram_tensor("out_dram", (P, FB, NT), mybir.dt.float32, kind="ExternalOutput").ap()
    build(nc, *args, out)
    r = run_bass_kernel_spmd(nc, [feeds], core_ids=[0])
    y = r.results[0]["out_dram"].reshape(P, FB, IMGS, TOK)
    return np.ascontiguousarray(y.transpose(2, 3, 1, 0)).reshape(IMGS, TOK, D)
```

```python
import concourse.bass as bass
from concourse import mybir
from contextlib import ExitStack

P = 128
D = 256
FB = D // P
IMGS, TOK = 16, 36
NT = IMGS * TOK
PATCH = 3 * 16 * 16
PK = PATCH // P
WARM = 12
PIECES = 3
CH = 2
CI = IMGS // CH
CT = NT // CH
TP = TOK + 1
PW = CI * TP
HK = 1024 // P
FF = 768
FK = FF // P
QB = 32
NQB = FF * D // P // QB
LN_EPS = 1e-5
NEG = -1e38
RND = 1.5 * 2.0 ** 23
WTOP = 1024.0
QMAX = 32767.0
TINY = 1e-12

VECS = ["L0_tok_b", "L0_attn_ln1_w", "L0_attn_ln1_b", "L0_attn_ln2_w", "L0_attn_ln2_b", "L0_attn_att_tmk",
        "L0_attn_att_tmv", "L0_attn_att_tmr", "L0_attn_time_decay", "L0_attn_time_first", "L0_attn_ffn_tmk",
        "L0_attn_ffn_tmr"]


def build(nc, patches_d, vecs_d, wtok_d, wk_d, wv_d, wr_d, wo_d, wrec_d, wkey_d, wval_d, wgate_d, wup_d,
          wdown_d, out_d):
    fp32, fp16 = mybir.dt.float32, mybir.dt.float16
    int16, uint16 = mybir.dt.int16, mybir.dt.uint16
    ALU = mybir.AluOpType
    ACT = mybir.ActivationFunctionType
    AX = mybir.AxisListType

    ctx = ExitStack()
    with ctx:
        def sb(name, *shape, dtype=fp32):
            return ctx.enter_context(nc.sbuf_tensor(name, list(shape), dtype))

        def sem(name):
            return ctx.enter_context(nc.semaphore(name))

        front = sb("front", P, PK * (NT + D))
        patches = front[:, 0:PK * NT].rearrange("p (c k t) -> p c k t", c=CH, k=PK)
        wtok = front[:, PK * NT:PK * (NT + D)].rearrange("p (k n) -> p k n", k=PK)
        hidden = front[:, 0:HK * NT].rearrange("p (k t) -> p k t", t=NT)
        vecs = sb("vecs", P, len(VECS), FB)
        wk, wv, wr, wo, wrec = (sb(n, P, FB, D) for n in ("wk", "wv", "wr", "wo", "wrec"))
        wkey = sb("wkey", P, FB, HK * P)
        wval = sb("wval", P, HK, D)
        ffn_raw = sb("ffn_raw", P, 3, FF * D // P)
        ffn_hi = sb("ffn_hi", P, 3, FF * D // P, dtype=fp16)
        ffn_lo = sb("ffn_lo", P, 3, FF * D // P, dtype=fp16)
        wgate, wup, wdown = (tuple(t[:, i, :].rearrange("p (k n) -> p k n", k=k) for t in (ffn_hi, ffn_lo))
                             for i, k in enumerate((FB, FB, FK)))
        tok_b, ln1_w, ln1_b, ln2_w, ln2_b, tmk, tmv, tmr, decay, first, ftmk, ftmr = (
            vecs[:, i, :] for i in range(len(VECS)))

        ident = sb("ident", P, P)
        mean_w = sb("mean_w", P, P)
        ones_row = sb("ones_row", 1, P)
        eps1 = sb("eps1", P, 1)
        eps2 = sb("eps2", P, 1)
        wneg = sb("wneg", P, FB)
        wseg = sb("wseg", P, FB, CI, TP)
        bmax = sb("bmax", P, 3, NQB)
        binv = sb("binv", P, 3, NQB)
        wrow = sb("wrow", P, 3, FK)
        wrinv = sb("wrinv", P, 3, FK)

        h = sb("h", P, FB, NT)
        dev = sb("dev", P, FB, NT)
        sq = sb("sq", P, FB, NT)
        lnr = sb("lnr", P, CH, 2, CT)
        x0 = sb("x0", P, FB, NT)
        hn = sb("hn", P, FB, IMGS, TP)
        dm = sb("dm", P, FB, NT)
        xk, xv, xr = (sb(n, P, FB, NT) for n in ("xk", "xv", "xr"))
        PT = FB * IMGS * TP
        arena = sb("arena", P, 12 * PT)

        def padded(i, n=1):
            return arena[:, i * PT:(i + n) * PT].rearrange("p (b i t) -> p b i t", i=IMGS, t=TP)

        kp = padded(0)
        pp = padded(1)
        ex = [padded(2 + j) for j in range(4)]
        ex01, ex23 = padded(2, 2), padded(4, 2)
        ev = padded(6)
        aa, bb = padded(7), padded(8)

        def plain(i):
            return arena[:, i * PT:i * PT + FB * NT].rearrange("p (b t) -> p b t", t=NT)

        v = plain(9)
        z = plain(10)
        ea = plain(11)
        num, den = sq, dm
        tmp = sb("tmp", P, FB, NT)

        def big(i):
            return arena[:, i * FK * NT:(i + 1) * FK * NT].rearrange("p (k t) -> p k t", t=NT)

        gate, up, sig = big(0), big(1), big(2)

        def half(t, n, dtype):
            w = FK * NT // 2
            return t[:, n * w:(n + 1) * w].bitcast(dtype).rearrange("p (k t) -> p k t", t=NT)

        gate_q, sig_q = half(arena, 6, int16), half(arena, 7, uint16)
        up_q, silu_q = half(front, 0, int16), half(front, 1, int16)
        prod_q, prod_hi, prod_lo = half(arena, 6, int16), half(arena, 7, fp16), half(arena, 0, fp16)
        x_q = sb("x_q", P, FB, NT, dtype=int16)
        x_hi = sb("x_hi", P, FB, NT, dtype=fp16)
        x_lo = sb("x_lo", P, FB, NT, dtype=fp16)
        mx = sb("mx", P, 5, FK)
        mx1 = sb("mx1", P, 5)
        top = sb("top", 1, 5)
        sc = sb("sc", P, 5)
        isc = sb("isc", P, 5)
        fac = sb("fac", P, 5)
        raw = sb("raw", P, 5)
        out_sc = sb("out_sc", P, FB)
        ps = ctx.enter_context(nc.psum_tensor("ps", [P, 8, 512], fp32))

        names = (["in_patch0_%d" % j for j in range(PIECES)] + ["in_wtok%d" % j for j in range(PIECES)]
                 + ["in_patch1"] + ["in_" + n for n in (
            "vecs", "wk", "wv", "wr", "wo", "wrec", "wkey", "wval", "ffn0", "ffn1", "ffn2")] + ["stored"])
        dma = {n: sem(n) for n in names}
        zeroed, const_ready, ident_ready = sem("zeroed"), sem("const_ready"), sem("ident_ready")
        wneg_ready, wseg_ready = sem("wneg_ready"), sem("wseg_ready")
        bmax_ready, bscale_ready, binv_ready = sem("bmax_ready"), sem("bscale_ready"), sem("binv_ready")
        wdiv_ready, wround_ready, wq_ready = sem("wdiv_ready"), sem("wround_ready"), sem("wq_ready")
        wrow_ready, wrinv_ready, brel_ready = sem("wrow_ready"), sem("wrinv_ready"), sem("brel_ready")
        wt_done, wt_hi_ready, wt_lo_ready = sem("wt_done"), sem("wt_hi_ready"), sem("wt_lo_ready")
        (tok_done, mean_done, var_done, k_done, v_done, r_done, o_done, rec_done, key_done, val_done) = (
            sem(n) for n in ("tok_done", "mean_done", "var_done", "k_done", "v_done", "r_done", "o_done",
                             "rec_done", "key_done", "val_done"))
        gate_done, up_done, down_done = sem("gate_done"), sem("up_done"), sem("down_done")
        h_ready, dev_ready, sq_ready, ln_ready, rstd_ready = (
            sem(n) for n in ("h_ready", "dev_ready", "sq_ready", "ln_ready", "rstd_ready"))
        norm_ready, x0_ready, hn_ready, dm_ready, mix_ready = (
            sem(n) for n in ("norm_ready", "x0_ready", "hn_ready", "dm_ready", "mix_ready"))
        kp_ready, v_ready, z_ready, abs_ready, ea_ready = (
            sem(n) for n in ("kp_ready", "v_ready", "z_ready", "abs_ready", "ea_ready"))
        pp_ready, arg01_ready, arg2_ready, arg3_ready, diff_ready, exp01_ready, exp23_ready = (
            sem(n) for n in ("pp_ready", "arg01_ready", "arg2_ready", "arg3_ready", "diff_ready", "exp01_ready", "exp23_ready"))
        num_ready = sem("num_ready")
        ev_ready, state_ready, n2_ready, part_ready, frac_ready = (
            sem(n) for n in ("ev_ready", "state_ready", "n2_ready", "part_ready", "frac_ready"))
        scaled_ready, lnden_ready, logq_ready, quot_ready, rw_ready = (
            sem(n) for n in ("scaled_ready", "lnden_ready", "logq_ready", "quot_ready", "rw_ready"))
        x1_ready, hx_ready, relu_ready, hid_ready = (
            sem(n) for n in ("x1_ready", "hx_ready", "relu_ready", "hid_ready"))
        soft_ready, logsig_ready, recsig_ready, gated_ready, h2_ready = (
            sem(n) for n in ("soft_ready", "logsig_ready", "recsig_ready", "gated_ready", "h2_ready"))
        mx_ready, mx1_ready, mxt_done, top_ready, topb_done, scale_step, scale_ready = (
            sem(n) for n in ("mx_ready", "mx1_ready", "mxt_done", "top_ready", "topb_done", "scale_step",
                             "scale_ready"))
        mxsilu_ready = sem("mxsilu_ready")
        xq_ready, xhi_ready, xlo_ready = sem("xq_ready"), sem("xhi_ready"), sem("xlo_ready")
        gate_ready, up_ready = sem("gate_ready"), sem("up_ready")
        gq_ready, sig_ready, sigq_ready, silu_ready = (
            sem(n) for n in ("gq_ready", "sig_ready", "sigq_ready", "silu_ready"))
        tq_ready, uq_ready, prod_ready, oq_ready, ohi_ready, olo_ready, out_sc_ready, out_ready = (
            sem(n) for n in ("tq_ready", "uq_ready", "prod_ready", "oq_ready", "ohi_ready", "olo_ready",
                             "out_sc_ready", "out_ready"))

        def cols(t, c):
            return t[:, :, c * CT:(c + 1) * CT]

        def imgs(t, c, b=None):
            t = cols(t, c) if b is None else t[:, b, c * CT:(c + 1) * CT]
            return t.rearrange("p b (i t) -> p b i t" if b is None else "p (i t) -> p i t", t=TOK)

        def now(t, c, b=None):
            s = slice(c * CI, (c + 1) * CI)
            return t[:, :, s, 1:TP] if b is None else t[:, b, s, 1:TP]

        def before(t, c, b=None):
            s = slice(c * CI, (c + 1) * CI)
            return t[:, :, s, 0:TOK] if b is None else t[:, b, s, 0:TOK]

        def run(t, c, b):
            return t[:, b, c * CI:(c + 1) * CI, :].rearrange("p i t -> p (i t)")

        def bank(n, count=1):
            return ps[:, n, 0:CT] if count == 1 else ps[:, n:n + count, 0:CT]

        def bank_imgs(n):
            return ps[:, n:n + 2, 0:CT].rearrange("p b (i t) -> p b i t", t=TOK)

        def twice(ap):
            return ap.unsqueeze(1).to_broadcast([P, FB, CT])

        TOKB, MEAN1, VAR1 = (0, 2), (4, 5), (6, 7)
        KB, VB, RB = (0, 6), (2, 0), (4, 2)
        WTB = (0, 1)
        OB, MEAN2, VAR2, RECB, KEYB, VALB = (6, 0), (2, 0), (3, 1), (4, 0), (2, 3), (6, 4)
        MEAN3, VAR3 = (6, 2), (7, 3)
        MEAN, VAR = (MEAN1, MEAN2, MEAN3), (VAR1, VAR2, VAR3)
        MXT, TOPB = 6, 7
        block = ctx.enter_context(nc.Block())

        @block.sync
        def _(sp):
            for j in range(PIECES):
                s = slice(j * PK // PIECES, (j + 1) * PK // PIECES)
                sp.dma_start(wtok[:, s, :], wtok_d[:, s, :]).then_inc(dma["in_wtok%d" % j], 16)
                sp.dma_start(patches[:, 0, s, :], patches_d[:, 0, s, :]).then_inc(dma["in_patch0_%d" % j], 16)
            sp.dma_start(patches[:, 1, :, :], patches_d[:, 1, :, :]).then_inc(dma["in_patch1"], 16)
            sp.dma_start(wk[:, :, :], wk_d).then_inc(dma["in_wk"], 16)
            sp.dma_start(wv[:, :, :], wv_d).then_inc(dma["in_wv"], 16)
            sp.dma_start(wr[:, :, :], wr_d).then_inc(dma["in_wr"], 16)
            sp.dma_start(wo[:, :, :], wo_d).then_inc(dma["in_wo"], 16)
            sp.dma_start(wrec[:, :, :], wrec_d).then_inc(dma["in_wrec"], 16)
            sp.dma_start(wkey[:, :, :], wkey_d).then_inc(dma["in_wkey"], 16)
            sp.dma_start(wval[:, :, :], wval_d).then_inc(dma["in_wval"], 16)
            for i, w in enumerate((wgate_d, wup_d, wdown_d)):
                sp.dma_start(ffn_raw[:, i, :], w).then_inc(dma["in_ffn%d" % i], 16)
            for c in range(CH):
                for m in range(FB):
                    sp.wait_ge(out_ready, FB * c + m + 1)
                    sp.dma_start(out_d[:, m, c * CT:(c + 1) * CT], x0[:, m, c * CT:(c + 1) * CT])\
                        .then_inc(dma["stored"], 16)
            sp.wait_ge(dma["stored"], 16 * CH * FB)

        @block.gpsimd
        def _(pool):
            pool.memset(ident[:, :], 0.0).then_inc(zeroed, 1)
            pool.memset(mean_w[:, :], 1.0 / D).then_inc(const_ready, 1)
            pool.memset(ones_row[:, :], 1.0).then_inc(const_ready, 1)
            pool.memset(eps1[:, :], LN_EPS).then_inc(const_ready, 1)
            pool.memset(eps2[:, :], LN_EPS * LN_EPS).then_inc(const_ready, 1)
            pool.wait_ge(zeroed, 1)
            pool.affine_select(out=ident[:, :], in_=ident[:, :], compare_op=ALU.not_equal, fill=1.0, base=0,
                               pattern=[[-1, P]], channel_multiplier=1).then_inc(ident_ready, 1)
            pool.memset(hn[:, :, :, 0:1], 0.0).then_inc(const_ready, 1)
            pool.memset(kp[:, :, :, 0:1], NEG).then_inc(const_ready, 1)
            for j in (0, 1):
                pool.memset(ex[j][:, :, :, 0:1], 0.0).then_inc(const_ready, 1)
            pool.memset(ev[:, :, :, 0:1], 0.0).then_inc(const_ready, 1)
            pool.memset(wseg[:, :, :, 0:1], NEG).then_inc(const_ready, 1)
            def divide(i):
                w3 = ffn_raw[:, i, :].rearrange("p (n q) -> p n q", q=QB)
                pool.wait_ge(binv_ready, i + 1)
                pool.tensor_tensor(w3, w3, binv[:, i, :].unsqueeze(2).to_broadcast([P, NQB, QB]),
                                   ALU.mult).then_inc(wdiv_ready, 1)

            def rescale(i):
                w3 = ffn_raw[:, i, :].rearrange("p (n q) -> p n q", q=QB)
                pool.wait_ge(wround_ready, i + 1)
                pool.wait_ge(brel_ready, i + 1)
                pool.tensor_tensor(w3, w3, bmax[:, i, :].unsqueeze(2).to_broadcast([P, NQB, QB]),
                                   ALU.mult).then_inc(wq_ready, 1)

            def bonus(c):
                pool.wait_ge(exp23_ready, c + 1)
                pool.wait_ge(v_ready, c + 1)
                pool.tensor_tensor(imgs(tmp, c), now(ex[3], c), imgs(v, c), ALU.mult).then_inc(n2_ready, 1)

            def outer_norm(c):
                pool.wait_ge(rstd_ready, c + 1)
                pool.tensor_tensor(cols(x0, c), cols(dev, c), twice(lnr[:, c, 0, :]), ALU.mult)\
                    .then_inc(x0_ready, 1)

            def bring(c):
                pool.wait_ge(exp01_ready, c + 1)
                pool.wait_ge(v_ready, c + 1)
                pool.tensor_tensor(now(ev, c), now(ex[1], c), imgs(v, c), ALU.mult).then_inc(ev_ready, 1)

            def numerator(c):
                pool.wait_ge(n2_ready, c + 1)
                pool.wait_ge(part_ready, 2 * c + 2)
                pool.tensor_tensor(cols(num, c), cols(num, c), cols(tmp, c), ALU.add).then_inc(num_ready, 1)

            outer_norm(0)
            outer_norm(1)
            bring(0)
            bonus(0)
            numerator(0)
            bring(1)
            bonus(1)
            numerator(1)

            def hx(c):
                pool.wait_ge(x1_ready, c + 1)
                pool.tensor_tensor(cols(h, c), cols(h, c), cols(x0, c), ALU.add).then_inc(hx_ready, 1)

            def squares(c):
                for m in range(HK):
                    pool.wait_ge(relu_ready, HK * c + m + 1)
                    t = hidden[:, m, c * CT:(c + 1) * CT]
                    pool.tensor_tensor(t, t, t, ALU.mult).then_inc(hid_ready, 1)

            hx(0)
            divide(0)
            divide(1)
            rescale(0)
            divide(2)
            rescale(1)
            squares(0)
            hx(1)
            rescale(2)
            squares(1)
            for m in range(FK):
                pool.wait_ge(sig_ready, m + 1)
                pool.tensor_scalar(sig_q[:, m, :], sig[:, m, :], 65536.0, 0.0, ALU.mult, ALU.add)\
                    .then_inc(sigq_ready, 1)

        @block.scalar
        def _(act):
            act.dma_start(vecs[:, :, :], vecs_d).then_inc(dma["in_vecs"], 16)
            act.preload_act_table_set("natural_log_exp_and_others")
            act.wait_ge(dma["in_vecs"], 16)
            act.activation(wneg[:, :], decay, ACT.Exp).then_inc(wneg_ready, 1)
            act.wait_ge(const_ready, 4)

            def embed(c, b):
                act.wait_ge(tok_done, FB * c + b + 1)
                act.activation(h[:, b, c * CT:(c + 1) * CT], bank(TOKB[c] + b), ACT.Identity,
                               bias=tok_b[:, b:b + 1]).then_inc(h_ready, 1)

            def square(n, c):
                act.wait_ge(dev_ready, CH * n + c + 1)
                act.activation(cols(sq, c), cols(dev, c), ACT.Square).then_inc(sq_ready, 1)

            def rstd(n, c):
                act.wait_ge(var_done, CH * n + c + 1)
                t = lnr[:, c, 0, :]
                act.activation(t, bank(VAR[n][c]), ACT.Ln, bias=eps1[:, :]).then_inc(ln_ready, 1)
                if n == 0:
                    act.activation(lnr[:, c, 1, :], bank(VAR[n][c]), ACT.Ln, bias=eps2[:, :],
                                   scale=1.0 + LN_EPS).then_inc(ln_ready, 1)
                    t = lnr[:, c, :, :]
                    act.wait_ge(ln_ready, 2 * (c + 1))
                else:
                    act.wait_ge(ln_ready, 2 * CH + CH * (n - 1) + c + 1)
                act.activation(t, t, ACT.Exp, scale=-0.5).then_inc(rstd_ready, 1)

            def affine(n, c):
                act.wait_ge(norm_ready, CH * n + c + 1)
                for b in range(FB):
                    w, o = ((ln1_w, ln1_b), (ln2_w, ln2_b))[n]
                    act.activation(now(hn, c, b), imgs(tmp if n == 0 else dev, c, b), ACT.Identity, bias=o[:, b:b + 1],
                                   scale=w[:, b:b + 1]).then_inc(hn_ready, 1)

            def key_out(c):
                act.wait_ge(k_done, c + 1)
                act.activation(now(kp, c), bank_imgs(KB[c]), ACT.Copy).then_inc(kp_ready, 1)

            def value_out(c):
                act.wait_ge(v_done, c + 1)
                act.activation(cols(v, c), bank(VB[c], 2), ACT.Copy).then_inc(v_ready, 1)

            def receptance_out(c):
                act.wait_ge(r_done, c + 1)
                act.activation(cols(z, c), bank(RB[c], 2), ACT.Copy).then_inc(z_ready, 1)
                act.activation(cols(ea, c), bank(RB[c], 2), ACT.Abs).then_inc(abs_ready, 1)
                act.wait_ge(abs_ready, c + 1)
                act.activation(cols(ea, c), cols(ea, c), ACT.Exp, scale=-1.0).then_inc(ea_ready, 1)

            def exps01(c):
                act.wait_ge(arg01_ready, c + 1)
                act.activation(now(ex01, c), now(ex01, c), ACT.Exp).then_inc(exp01_ready, 1)

            def exps23(c):
                act.wait_ge(diff_ready, FB * (c + 1))
                act.activation(now(ex[2], c), now(ex[3], c), ACT.Relu).then_inc(arg2_ready, 1)
                act.wait_ge(arg2_ready, c + 1)
                act.activation(now(ex[3], c), now(ex[3], c), ACT.Relu, scale=-1.0).then_inc(arg3_ready, 1)
                act.wait_ge(arg3_ready, c + 1)
                act.activation(now(ex23, c), now(ex23, c), ACT.Exp, scale=-1.0).then_inc(exp23_ready, 1)

            def lnden(c):
                act.wait_ge(scaled_ready, c + 1)
                act.activation(cols(den, c), cols(den, c), ACT.Ln).then_inc(lnden_ready, 1)

            def quot(c):
                act.wait_ge(logq_ready, c + 1)
                act.activation(cols(den, c), cols(den, c), ACT.Exp).then_inc(quot_ready, 1)

            def weights_out(g0, g1):
                flat = ffn_hi[:, :, :].rearrange("p a b -> p (a b)")
                for g in range(g0, g1):
                    act.wait_ge(wt_done, g + 1)
                    act.activation(flat[:, g * 512:(g + 1) * 512], ps[:, WTB[g % 2], :], ACT.Copy)\
                        .then_inc(wt_hi_ready, 1)

            def soft(c):
                act.wait_ge(rec_done, c + 1)
                act.wait_ge(logq_ready, c + 1)
                act.wait_ge(scaled_ready, c + 1)
                act.activation(cols(z, c), bank(RECB[c], 2), ACT.Copy).then_inc(z_ready, 1)
                act.activation(cols(ea, c), bank(RECB[c], 2), ACT.Abs).then_inc(abs_ready, 1)
                act.wait_ge(abs_ready, CH + c + 1)
                act.activation(cols(ea, c), cols(ea, c), ACT.Exp, scale=-1.0).then_inc(ea_ready, 1)
                act.wait_ge(ea_ready, CH + c + 1)
                act.activation(cols(ea, c), cols(ea, c), ACT.Ln, bias=1.0).then_inc(soft_ready, 1)

            def recsig(c):
                act.wait_ge(logsig_ready, c + 1)
                act.activation(cols(ea, c), cols(ea, c), ACT.Exp).then_inc(recsig_ready, 1)

            def relu(c, m):
                act.wait_ge(key_done, HK * c + m + 1)
                if c == 0 and m == 0:
                    act.wait_ge(tok_done, FB * CH)
                act.activation(hidden[:, m, c * CT:(c + 1) * CT], bank(KEYB[m % 2]), ACT.Relu)\
                    .then_inc(relu_ready, 1)

            embed(0, 0)
            embed(0, 1)
            square(0, 0)
            embed(1, 0)
            rstd(0, 0)
            affine(0, 0)
            embed(1, 1)
            square(0, 1)
            key_out(0)
            rstd(0, 1)
            value_out(0)
            exps01(0)
            affine(0, 1)
            exps23(0)
            receptance_out(0)
            key_out(1)
            lnden(0)
            quot(0)
            value_out(1)
            receptance_out(1)
            exps01(1)
            exps23(1)
            square(1, 0)
            lnden(1)
            quot(1)
            rstd(1, 0)
            affine(1, 0)
            square(1, 1)
            soft(0)
            relu(0, 0)
            relu(0, 1)
            rstd(1, 1)
            relu(0, 2)
            recsig(0)
            affine(1, 1)
            for m in range(3, HK):
                relu(0, m)
            soft(1)
            relu(1, 0)
            recsig(1)
            for m in range(1, 4):
                relu(1, m)
            square(2, 0)
            for m in range(4, 6):
                relu(1, m)
            rstd(2, 0)
            for m in range(6, HK):
                relu(1, m)
            weights_out(0, 2)
            square(2, 1)
            weights_out(2, 5)
            rstd(2, 1)
            weights_out(5, 9)
            act.preload_act_table_set("sigmoid_and_others")

            def evacuate(dst, i, done, ready, m):
                for c in range(CH):
                    act.wait_ge(done, CH * m + c + 1)
                    act.activation(dst[:, m, c * CT:(c + 1) * CT], bank((CH * m + c) % 6), ACT.Copy,
                                   scale=wrow[:, i, m:m + 1]).then_inc(ready, 1)

            def to_int(dst, src, i, m, ready):
                act.activation(dst[:, m, :], src[:, m, :], ACT.Copy, scale=fac[:, i:i + 1]).then_inc(ready, 1)

            act.wait_ge(wrow_ready, 3 * 2)
            for m in range(FK):
                evacuate(gate, 0, gate_done, gate_ready, m)
            act.wait_ge(scale_ready, 2)
            for m in range(FK):
                to_int(gate_q, gate, 1, m, gq_ready)
                evacuate(up, 1, up_done, up_ready, m)
                act.wait_ge(gq_ready, m + 1)
                act.activation(sig[:, m, :], gate_q[:, m, :], ACT.Sigmoid, scale=sc[:, 1:2])\
                    .then_inc(sig_ready, 1)
            act.wait_ge(scale_ready, 3)
            for m in range(FK):
                to_int(up_q, up, 2, m, uq_ready)
            act.wait_ge(scale_ready, 4)
            for m in range(FK):
                to_int(silu_q, sig, 3, m, tq_ready)
            act.wait_ge(scale_ready, 5)
            for m in range(FK):
                to_int(prod_q, up, 4, m, oq_ready)

        @block.vector
        def _(dve):
            def round_weights(i):
                dve.wait_ge(dma["in_ffn%d" % i], 16)
                w3 = ffn_raw[:, i, :].rearrange("p (n q) -> p n q", q=QB)
                dve.tensor_reduce(bmax[:, i, :], w3, AX.X, ALU.max, apply_absolute_value=True)\
                    .then_inc(bmax_ready, 1)
                dve.wait_ge(bmax_ready, i + 1)
                dve.tensor_scalar(bmax[:, i, :], bmax[:, i, :], 1.0 / 7.0, TINY, ALU.mult, ALU.max)\
                    .then_inc(bscale_ready, 1)
                dve.wait_ge(bscale_ready, i + 1)
                dve.reciprocal(binv[:, i, :], bmax[:, i, :]).then_inc(binv_ready, 1)

            def row_scales(i):
                blocks = FK if i < 2 else FB
                s3 = bmax[:, i, :].rearrange("p (m n) -> p m n", m=blocks)
                dve.tensor_reduce(wrow[:, i, 0:blocks], s3, AX.X, ALU.max).then_inc(wrow_ready, 1)
                dve.wait_ge(wrow_ready, 2 * i + 1)
                dve.reciprocal(wrinv[:, i, 0:blocks], wrow[:, i, 0:blocks]).then_inc(wrinv_ready, 1)
                dve.wait_ge(wrinv_ready, i + 1)
                dve.scalar_tensor_tensor(s3, s3, WTOP, wrinv[:, i, 0:blocks].unsqueeze(2)
                                         .to_broadcast([P, blocks, NQB // blocks]), ALU.mult, ALU.mult)\
                    .then_inc(brel_ready, 1)
                dve.tensor_scalar(wrow[:, i, 0:blocks], wrow[:, i, 0:blocks], 1.0 / WTOP, None, ALU.mult)\
                    .then_inc(wrow_ready, 1)

            def weights_low(g0, g1):
                flat, low = (t[:, :, :].rearrange("p a b -> p (a b)") for t in (ffn_hi, ffn_lo))
                for g in range(g0, g1):
                    s = slice(g * 512, (g + 1) * 512)
                    dve.wait_ge(wt_hi_ready, g + 1)
                    dve.tensor_tensor(low[:, s], ps[:, WTB[g % 2], :], flat[:, s], ALU.subtract)\
                        .then_inc(wt_lo_ready, 1)

            def round_weights2(i):
                dve.wait_ge(wdiv_ready, i + 1)
                dve.tensor_scalar(ffn_raw[:, i, :], ffn_raw[:, i, :], RND, RND, ALU.add, ALU.subtract)\
                    .then_inc(wround_ready, 1)

            def deviation(n, c):
                src = x0 if n == 1 else h
                dve.wait_ge(mean_done, CH * n + c + 1)
                dve.tensor_tensor(cols(dev, c), cols(src, c), twice(bank(MEAN[n][c])), ALU.subtract)\
                    .then_inc(dev_ready, 1)

            def normalise(n, c):
                dve.wait_ge(rstd_ready, CH * n + c + 1)
                dst = tmp if n == 0 else dev
                dve.tensor_tensor(cols(dst, c), cols(dev, c), twice(lnr[:, c, 1 if n == 0 else 0, :]), ALU.mult)\
                    .then_inc(norm_ready, 1)

            def shift(n, c):
                dve.wait_ge(hn_ready, FB * (CH * n + c + 1))
                if n == 1:
                    dve.wait_ge(rw_ready, c + 1)
                dve.tensor_tensor(imgs(dm, c), now(hn, c), before(hn, c), ALU.subtract).then_inc(dm_ready, 1)

            def mix(n, c, j):
                dve.wait_ge(dm_ready, CH * n + c + 1)
                dst, m = (((xk, tmk), (xv, tmv), (xr, tmr)) if n == 0 else ((xr, ftmr), (xk, ftmk)))[j]
                for b in range(FB):
                    dve.scalar_tensor_tensor(imgs(dst, c, b), imgs(dm, c, b), m[:, b:b + 1],
                                             before(hn, c, b), ALU.mult, ALU.add).then_inc(mix_ready, 1)

            def maxima(c):
                dve.wait_ge(kp_ready, c + 1)
                for b in range(FB):
                    dve.tensor_tensor_scan(run(pp, c, b), wseg[:, b, :, :].rearrange("p i t -> p (i t)"),
                                           run(kp, c, b), NEG, ALU.add, ALU.max).then_inc(pp_ready, 1)

            def exponents(c):
                dve.wait_ge(pp_ready, FB * (c + 1))
                for b in range(FB):
                    dve.scalar_tensor_tensor(now(ex[0], c, b), before(pp, c, b), wneg[:, b:b + 1],
                                             now(pp, c, b), ALU.add, ALU.subtract)
                dve.tensor_tensor(now(ex[1], c), now(kp, c), now(pp, c), ALU.subtract).then_inc(arg01_ready, 1)

            def bonus_exponents(c):
                for b in range(FB):
                    dve.scalar_tensor_tensor(now(ex[3], c, b), now(kp, c, b), first[:, b:b + 1],
                                             before(pp, c, b), ALU.add, ALU.subtract).then_inc(diff_ready, 1)

            def weight_state(c):
                dve.wait_ge(exp01_ready, c + 1)
                for b in range(FB):
                    dve.tensor_tensor_scan(run(bb, c, b), run(ex[0], c, b), run(ex[1], c, b), 0.0,
                                           ALU.mult, ALU.add).then_inc(state_ready, 1)

            def value_state(c):
                dve.wait_ge(ev_ready, c + 1)
                for b in range(FB):
                    dve.tensor_tensor_scan(run(aa, c, b), run(ex[0], c, b), run(ev, c, b), 0.0,
                                           ALU.mult, ALU.add).then_inc(state_ready, 1)

            def fraction(c):
                dve.wait_ge(exp23_ready, c + 1)
                dve.wait_ge(state_ready, 2 * FB * (c + 1))
                dve.tensor_tensor(imgs(den, c), now(ex[2], c), before(bb, c), ALU.mult).then_inc(part_ready, 1)
                dve.tensor_tensor(imgs(num, c), now(ex[2], c), before(aa, c), ALU.mult).then_inc(part_ready, 1)
                dve.wait_ge(part_ready, 2 * c + 1)
                dve.tensor_tensor(imgs(den, c), imgs(den, c), now(ex[3], c), ALU.add).then_inc(frac_ready, 1)
                dve.wait_ge(frac_ready, c + 1)
                dve.wait_ge(ea_ready, c + 1)
                dve.scalar_tensor_tensor(cols(den, c), cols(ea, c), 1.0, cols(den, c), ALU.add, ALU.mult)\
                    .then_inc(scaled_ready, 1)

            def logq(c):
                dve.wait_ge(lnden_ready, c + 1)
                dve.scalar_tensor_tensor(cols(den, c), cols(z, c), 0.0, cols(den, c), ALU.min, ALU.subtract)\
                    .then_inc(logq_ready, 1)

            def rwkv(c):
                dve.wait_ge(quot_ready, c + 1)
                dve.wait_ge(num_ready, c + 1)
                dve.tensor_tensor(cols(xk, c), cols(num, c), cols(den, c), ALU.mult).then_inc(rw_ready, 1)

            def residual(c):
                dve.wait_ge(o_done, c + 1)
                dve.tensor_tensor(cols(x0, c), cols(x0, c), bank(OB[c], 2), ALU.add).then_inc(x1_ready, 1)

            def logsig(c):
                dve.wait_ge(soft_ready, c + 1)
                dve.scalar_tensor_tensor(cols(ea, c), cols(z, c), 0.0, cols(ea, c), ALU.min, ALU.subtract)\
                    .then_inc(logsig_ready, 1)

            def channel_out(c):
                dve.wait_ge(recsig_ready, c + 1)
                dve.wait_ge(hx_ready, c + 1)
                s = slice(c * CT, (c + 1) * CT)
                for b in range(FB):
                    dve.wait_ge(val_done, FB * c + b + 1)
                    dve.tensor_tensor(xv[:, b, s], ea[:, b, s], bank(VALB[c] + b), ALU.mult)\
                        .then_inc(gated_ready, 1)
                    dve.wait_ge(gated_ready, FB * c + b + 1)
                    dve.tensor_tensor(h[:, b, s], h[:, b, s], xv[:, b, s], ALU.add).then_inc(h2_ready, 1)

            dve.wait_ge(wneg_ready, 1)
            dve.tensor_scalar(wneg[:, :], wneg[:, :], -1.0, None, ALU.mult).then_inc(wneg_ready, 1)
            dve.wait_ge(wneg_ready, 2)
            dve.memset(wseg[:, :, :, 1:TP], 0.0).then_inc(wseg_ready, 1)
            dve.wait_ge(wseg_ready, 1)
            for b in range(FB):
                dve.tensor_scalar(wseg[:, b, :, 1:TP], wseg[:, b, :, 1:TP], wneg[:, b:b + 1], None, ALU.add)\
                    .then_inc(wseg_ready, 1)
            dve.wait_ge(wseg_ready, 1 + FB)
            deviation(0, 0)
            normalise(0, 0)
            dve.wait_ge(const_ready, 10)
            shift(0, 0)
            mix(0, 0, 0)
            deviation(0, 1)
            mix(0, 0, 1)
            mix(0, 0, 2)
            maxima(0)
            exponents(0)
            bonus_exponents(0)
            normalise(0, 1)
            weight_state(0)
            shift(0, 1)
            mix(0, 1, 0)
            value_state(0)
            mix(0, 1, 1)
            mix(0, 1, 2)
            fraction(0)
            maxima(1)
            logq(0)
            exponents(1)
            rwkv(0)
            bonus_exponents(1)
            round_weights(0)
            weight_state(1)
            value_state(1)
            residual(0)
            fraction(1)
            deviation(1, 0)
            logq(1)
            round_weights(1)
            normalise(1, 0)
            rwkv(1)
            row_scales(0)
            shift(1, 0)
            mix(1, 0, 0)
            mix(1, 0, 1)
            round_weights2(0)
            row_scales(1)
            residual(1)
            deviation(1, 1)
            round_weights(2)
            row_scales(2)
            round_weights2(1)
            logsig(0)
            normalise(1, 1)
            shift(1, 1)
            mix(1, 1, 0)
            mix(1, 1, 1)
            round_weights2(2)
            channel_out(0)
            logsig(1)
            deviation(2, 0)
            normalise(2, 0)
            dve.wait_ge(norm_ready, 2 * CH + 1)
            dve.tensor_reduce(mx[:, 0, 0:1], cols(dev, 0), AX.XY, ALU.max, apply_absolute_value=True)\
                .then_inc(mx_ready, 1)
            channel_out(1)
            weights_low(0, 2)
            deviation(2, 1)
            weights_low(2, 5)
            normalise(2, 1)
            dve.wait_ge(norm_ready, 2 * CH + 2)
            dve.tensor_reduce(mx[:, 0, 1:2], cols(dev, 1), AX.XY, ALU.max, apply_absolute_value=True)\
                .then_inc(mx_ready, 1)

            def reduce_max(i, count, ready, seen):
                dve.wait_ge(ready, seen)
                dve.tensor_reduce(mx1[:, i:i + 1], mx[:, i, 0:count], AX.X, ALU.max).then_inc(mx1_ready, 1)

            def core_max(i):
                dve.wait_ge(mxt_done, i + 1)
                dve.tensor_reduce(top[0:1, i:i + 1], ps[0:1, MXT, 0:P], AX.X, ALU.max).then_inc(top_ready, 1)

            steps = [0]

            def small(ins):
                steps[0] += 1
                ins.then_inc(scale_step, 1)
                dve.wait_ge(scale_step, steps[0])

            def scale(i, one):
                dve.wait_ge(topb_done, i + 1)
                if one is None:
                    small(dve.tensor_scalar(sc[:, i:i + 1], ps[:, TOPB, 0:1], 1.0 / QMAX, TINY, ALU.mult, ALU.max))
                    dve.reciprocal(fac[:, i:i + 1], sc[:, i:i + 1]).then_inc(scale_ready, 1)
                    return
                small(dve.tensor_scalar(raw[:, i:i + 1], ps[:, TOPB, 0:1], one, 1.0 / QMAX, ALU.mult, ALU.mult))
                small(dve.tensor_scalar(sc[:, i:i + 1], raw[:, i:i + 1], TINY, None, ALU.max))
                small(dve.reciprocal(isc[:, i:i + 1], sc[:, i:i + 1]))
                dve.tensor_scalar(fac[:, i:i + 1], isc[:, i:i + 1], one, None, ALU.mult).then_inc(scale_ready, 1)

            reduce_max(0, CH, mx_ready, CH)
            weights_low(5, 9)
            core_max(0)
            scale(0, None)
            dve.wait_ge(scale_ready, 1)
            for c in range(CH):
                dve.tensor_scalar(cols(x_q, c), cols(dev, c), fac[:, 0:1], None, ALU.mult).then_inc(xq_ready, 1)
                dve.wait_ge(xq_ready, c + 1)
                dve.tensor_copy(cols(x_hi, c), cols(x_q, c)).then_inc(xhi_ready, 1)
                dve.wait_ge(xhi_ready, c + 1)
                dve.tensor_tensor(cols(x_lo, c), cols(x_q, c), cols(x_hi, c), ALU.subtract).then_inc(xlo_ready, 1)
            for m in range(FK):
                dve.wait_ge(gate_ready, CH * (m + 1))
                dve.tensor_reduce(mx[:, 1, m:m + 1], gate[:, m, :], AX.X, ALU.max, apply_absolute_value=True)\
                    .then_inc(mx_ready, 1)
            reduce_max(1, FK, mx_ready, CH + FK)
            core_max(1)
            scale(1, sc[:, 0:1])
            for m in range(FK + 1):
                if m < FK:
                    dve.wait_ge(up_ready, CH * (m + 1))
                    dve.tensor_reduce(mx[:, 2, m:m + 1], up[:, m, :], AX.X, ALU.max, apply_absolute_value=True)\
                        .then_inc(mx_ready, 1)
                if m == FK - 1:
                    reduce_max(2, FK, mx_ready, CH + 2 * FK)
                if m == FK:
                    core_max(2)
                    scale(2, sc[:, 0:1])
                j = m - 1
                if j >= 0:
                    dve.wait_ge(sigq_ready, j + 1)
                    dve.tensor_tensor(sig[:, j, :], sig_q[:, j, :], gate_q[:, j, :], ALU.mult)\
                        .then_inc(silu_ready, 1)
                    dve.wait_ge(silu_ready, j + 1)
                    dve.tensor_reduce(mx[:, 3, j:j + 1], sig[:, j, :], AX.X, ALU.max, apply_absolute_value=True)\
                        .then_inc(mxsilu_ready, 1)
            reduce_max(3, FK, mxsilu_ready, FK)
            core_max(3)
            small(dve.tensor_scalar(raw[:, 0:1], sc[:, 1:2], 1.0 / 65536.0, None, ALU.mult))
            scale(3, raw[:, 0:1])
            for m in range(FK):
                dve.wait_ge(uq_ready, m + 1)
                dve.wait_ge(tq_ready, m + 1)
                dve.tensor_tensor(up[:, m, :], silu_q[:, m, :], up_q[:, m, :], ALU.mult).then_inc(prod_ready, 1)
                dve.wait_ge(prod_ready, m + 1)
                dve.tensor_reduce(mx[:, 4, m:m + 1], up[:, m, :], AX.X, ALU.max, apply_absolute_value=True)\
                    .then_inc(mx_ready, 1)
            reduce_max(4, FK, mx_ready, CH + 3 * FK)
            core_max(4)
            small(dve.tensor_scalar(mx1[:, 0:1], sc[:, 2:3], sc[:, 3:4], None, ALU.mult))
            scale(4, mx1[:, 0:1])
            dve.tensor_scalar(out_sc[:, :], wrow[:, 2, 0:FB], sc[:, 4:5], None, ALU.mult).then_inc(out_sc_ready, 1)
            for m in range(FK):
                dve.wait_ge(oq_ready, m + 1)
                dve.tensor_copy(prod_hi[:, m, :], prod_q[:, m, :]).then_inc(ohi_ready, 1)
                dve.wait_ge(ohi_ready, m + 1)
                dve.tensor_tensor(prod_lo[:, m, :], prod_q[:, m, :], prod_hi[:, m, :], ALU.subtract)\
                    .then_inc(olo_ready, 1)
            dve.wait_ge(out_sc_ready, 1)
            for c in range(CH):
                for m in range(FB):
                    dve.wait_ge(down_done, FB * c + m + 1)
                    s = slice(c * CT, (c + 1) * CT)
                    dve.scalar_tensor_tensor(x0[:, m, s], bank(FB * c + m), out_sc[:, m:m + 1], h[:, m, s],
                                             ALU.mult, ALU.add).then_inc(out_ready, 1)

        @block.tensor
        def _(pe):
            def product(dst, w, src, m, c, blocks, rhs=None):
                for k in range(blocks):
                    r = src[:, k, c * CT:(c + 1) * CT] if rhs is None else rhs(k)
                    last = pe.matmul(dst, w[:, k, m * P:(m + 1) * P], r, start=(k == 0), stop=(k == blocks - 1))
                return last

            def embed(c, m):
                for k in range(PK):
                    if c == 0 and m == 0 and k * PIECES % PK == 0:
                        pe.wait_ge(dma["in_wtok%d" % (k * PIECES // PK)], 16)
                        pe.wait_ge(dma["in_patch0_%d" % (k * PIECES // PK)], 16)
                    if c == 1 and m == 0 and k == 0:
                        pe.wait_ge(dma["in_patch1"], 16)
                    last = pe.matmul(bank(TOKB[c] + m), wtok[:, k, m * P:(m + 1) * P], patches[:, c, k, :],
                                     start=(k == 0), stop=(k == PK - 1))
                last.then_inc(tok_done, 1)

            def spread(dst, src, c):
                for k in range(FB):
                    last = pe.matmul(dst, mean_w[:, :], src[:, k, c * CT:(c + 1) * CT], start=(k == 0),
                                     stop=(k == FB - 1))
                return last

            def project(w, src, banks, done, c):
                for m in range(FB):
                    last = product(bank(banks[c] + m), w, src, m, c, FB)
                last.then_inc(done, 1)

            def key_head(c):
                if c == 0:
                    pe.wait_ge(dma["in_wk"], 16)
                    pe.wait_ge(h_ready, FB * CH)
                else:
                    pe.wait_ge(ln_ready, 2 * CH)
                pe.wait_ge(mix_ready, 3 * FB * c + FB)
                project(wk, xk, KB, k_done, c)

            def value_head(c):
                if c == 0:
                    pe.wait_ge(dma["in_wv"], 16)
                else:
                    pe.wait_ge(kp_ready, 1)
                pe.wait_ge(mix_ready, 3 * FB * c + 2 * FB)
                project(wv, xv, VB, v_done, c)

            def receptance_head(c):
                if c == 0:
                    pe.wait_ge(dma["in_wr"], 16)
                    pe.wait_ge(dev_ready, CH)
                else:
                    pe.wait_ge(v_ready, 1)
                pe.wait_ge(mix_ready, 3 * FB * (c + 1))
                project(wr, xr, RB, r_done, c)

            def weights(g0, g1):
                for g in range(g0, g1):
                    i = g // 3
                    pe.wait_ge(wq_ready, i + 1)
                    if g == 0:
                        pe.wait_ge(ident_ready, 1)
                        pe.wait_ge(z_ready, 2 * CH)
                        pe.wait_ge(abs_ready, 2 * CH)
                    if g >= 2:
                        pe.wait_ge(wt_lo_ready, g - 1)
                    kb, mb = (FB, FK) if i < 2 else (FK, FB)
                    for j in range(4):
                        k, m = divmod(4 * (g % 3) + j, mb)
                        last = pe.transpose(ps[:, WTB[g % 2], j * P:(j + 1) * P],
                                            ffn_raw[:, i, (m * kb + k) * P:(m * kb + k + 1) * P], ident[:, :])
                    last.then_inc(wt_done, 1)

            def wkv_out(c):
                if c == 0:
                    pe.wait_ge(dma["in_wo"], 16)
                pe.wait_ge(kp_ready, CH)
                pe.wait_ge(v_ready, CH)
                pe.wait_ge(rw_ready, c + 1)
                project(wo, xk, OB, o_done, c)

            def warm(count):
                for _ in range(count):
                    pe.matmul(ps[:, 7, 0:P], mean_w[:, :], mean_w[:, :], start=True, stop=True)

            def mean1(c):
                pe.wait_ge(h_ready, FB * (c + 1))
                spread(bank(MEAN1[c]), h, c).then_inc(mean_done, 1)

            def var1(c):
                pe.wait_ge(sq_ready, c + 1)
                spread(bank(VAR1[c]), sq, c).then_inc(var_done, 1)

            pe.wait_ge(const_ready, 1)
            warm(WARM)
            embed(0, 0)
            embed(0, 1)
            mean1(0)
            embed(1, 0)
            var1(0)
            embed(1, 1)
            mean1(1)
            key_head(0)
            var1(1)
            value_head(0)
            receptance_head(0)
            key_head(1)
            value_head(1)
            receptance_head(1)

            def mean2(c):
                pe.wait_ge(x1_ready, c + 1)
                if c == 0:
                    pe.wait_ge(z_ready, CH)
                    pe.wait_ge(abs_ready, CH)
                spread(bank(MEAN2[c]), x0, c).then_inc(mean_done, 1)

            def var2(c):
                pe.wait_ge(sq_ready, CH + c + 1)
                spread(bank(VAR2[c]), sq, c).then_inc(var_done, 1)

            def receptance(c):
                if c == 0:
                    pe.wait_ge(dma["in_wrec"], 16)
                    pe.wait_ge(z_ready, 1)
                    pe.wait_ge(abs_ready, 1)
                else:
                    pe.wait_ge(dev_ready, CH + 2)
                    pe.wait_ge(ln_ready, 3 * CH)
                pe.wait_ge(mix_ready, 3 * FB * CH + 2 * FB * c + FB)
                project(wrec, xr, RECB, rec_done, c)

            def keys(c, m0, m1):
                if (c, m0) == (0, 0):
                    pe.wait_ge(dma["in_wkey"], 16)
                    pe.wait_ge(dev_ready, CH + 1)
                    pe.wait_ge(ln_ready, 2 * CH + 1)
                pe.wait_ge(mix_ready, 3 * FB * CH + 2 * FB * (c + 1))
                for m in range(m0, m1):
                    n = HK * c + m
                    if n >= 2:
                        pe.wait_ge(relu_ready, n - 1)
                    product(bank(KEYB[m % 2]), wkey, xk, m, c, FB).then_inc(key_done, 1)

            def values(c):
                if c == 0:
                    pe.wait_ge(dma["in_wval"], 16)
                else:
                    pe.wait_ge(z_ready, CH + 1)
                    pe.wait_ge(abs_ready, CH + 1)
                for m in range(FB):
                    for k in range(HK):
                        if m == 0:
                            pe.wait_ge(hid_ready, HK * c + k + 1)
                        last = pe.matmul(bank(VALB[c] + m), wval[:, k, m * P:(m + 1) * P],
                                         hidden[:, k, c * CT:(c + 1) * CT], start=(k == 0), stop=(k == HK - 1))
                    last.then_inc(val_done, 1)

            def mean3(c):
                pe.wait_ge(h2_ready, FB * (c + 1))
                if c == 1:
                    pe.wait_ge(relu_ready, HK * CH)
                spread(bank(MEAN3[c]), h, c).then_inc(mean_done, 1)

            def var3(c):
                pe.wait_ge(sq_ready, 2 * CH + c + 1)
                spread(bank(VAR3[c]), sq, c).then_inc(var_done, 1)

            wkv_out(0)
            mean2(0)
            var2(0)
            wkv_out(1)
            mean2(1)
            receptance(0)
            keys(0, 0, 2)
            var2(1)
            keys(0, 2, HK)
            values(0)
            receptance(1)
            keys(1, 0, 4)
            mean3(0)
            keys(1, 4, 6)
            var3(0)
            keys(1, 6, HK)
            values(1)
            weights(0, 2)
            mean3(1)
            weights(2, 5)
            var3(1)
            weights(5, 9)

            def spread_max(i):
                pe.wait_ge(mx1_ready, i + 1)
                if i == 0:
                    pe.wait_ge(dev_ready, 3 * CH)
                    pe.wait_ge(ln_ready, 4 * CH)
                    pe.wait_ge(const_ready, 2)
                else:
                    pe.wait_ge(scale_ready, i)
                pe.transpose(ps[0:1, MXT, 0:P], mx1[:, i:i + 1], ident[:, :]).then_inc(mxt_done, 1)
                pe.wait_ge(top_ready, i + 1)
                pe.matmul(ps[:, TOPB, 0:1], ones_row[0:1, :], top[0:1, i:i + 1], start=True, stop=True)\
                    .then_inc(topb_done, 1)

            def split_product(dst, w, hi, lo, k, m, c, start, stop):
                ws, cs = slice(m * P, (m + 1) * P), slice(c * CT, (c + 1) * CT)
                pe.matmul(dst, w[0][:, k, ws], hi[:, k, cs], start=start, stop=False)
                pe.matmul(dst, w[0][:, k, ws], lo[:, k, cs], start=False, stop=False)
                return pe.matmul(dst, w[1][:, k, ws], hi[:, k, cs], start=False, stop=stop)

            def expand(w, done, ready, before_ready):
                for m in range(FK):
                    for c in range(CH):
                        n = CH * m + c
                        if n < 6 and before_ready is not None:
                            pe.wait_ge(before_ready, CH * FK - 6 + n + 1)
                        if n >= 6:
                            pe.wait_ge(ready, n - 5)
                        if m == 0 and w is wgate:
                            pe.wait_ge(xlo_ready, c + 1)
                        for k in range(FB):
                            last = split_product(bank(n % 6), w, x_hi, x_lo, k, m, c, k == 0, k == FB - 1)
                        last.then_inc(done, 1)

            spread_max(0)
            pe.wait_ge(wt_lo_ready, 9)
            expand(wgate, gate_done, gate_ready, None)
            spread_max(1)
            expand(wup, up_done, up_ready, gate_ready)
            spread_max(2)
            spread_max(3)
            spread_max(4)
            pe.wait_ge(up_ready, CH * FK)
            for k in range(FK):
                pe.wait_ge(olo_ready, k + 1)
                for c in range(CH):
                    for m in range(FB):
                        last = split_product(bank(FB * c + m), wdown, prod_hi, prod_lo, k, m, c, k == 0, k == FK - 1)
                        if k == FK - 1:
                            last.then_inc(down_done, 1)


def kernel(**inputs):
    import numpy as np
    import concourse.bacc as bacc
    from concourse.bass_utils import run_bass_kernel_spmd

    def inner(w):
        return w.reshape(-1, P, w.shape[1]).transpose(1, 0, 2)

    def outer(w):
        return w.reshape(-1, P, w.shape[1]).transpose(1, 0, 2).reshape(P, -1)

    g = {n: np.asarray(a) for n, a in inputs.items()}
    side = g["x"].shape[-1] // 16
    x = g["x"].reshape(IMGS, 3, side, 16, side, 16).transpose(1, 3, 5, 0, 2, 4)
    arrays = {
        "patches": x.reshape(PK, P, CH, CT).transpose(1, 2, 0, 3),
        "vecs": np.stack([g[n].reshape(FB, P) for n in VECS]).transpose(2, 0, 1),
        "wtok": inner(g["L0_tok_W"].T),
        "wk": inner(g["L0_attn_Wk"].T), "wv": inner(g["L0_attn_Wv"].T), "wr": inner(g["L0_attn_Wr"].T),
        "wo": inner(g["L0_attn_Wo"].T), "wrec": inner(g["L0_attn_Wrec"].T), "wkey": inner(g["L0_attn_Wkey"].T),
        "wval": inner(g["L0_attn_Wval"].T),
        "wgate": outer(g["L0_ffn_w_gate"]), "wup": outer(g["L0_ffn_w_up"]), "wdown": outer(g["L0_ffn_w_down"]),
    }
    nc = bacc.Bacc("TRN2", target_bir_lowering=False, num_devices=1)
    feeds, args = {}, []
    for name, a in arrays.items():
        feeds[name + "_dram"] = np.ascontiguousarray(a)
        args.append(nc.dram_tensor(name + "_dram", a.shape, mybir.dt.float32, kind="ExternalInput").ap())
    out = nc.dram_tensor("out_dram", (P, FB, NT), mybir.dt.float32, kind="ExternalOutput").ap()
    build(nc, *args, out)
    r = run_bass_kernel_spmd(nc, [feeds], core_ids=[0])
    y = r.results[0]["out_dram"].reshape(P, FB, IMGS, TOK)
    return np.ascontiguousarray(y.transpose(2, 3, 1, 0)).reshape(IMGS, TOK, D)
```

```python
import concourse.bass as bass
from concourse import mybir
from contextlib import ExitStack

P = 128
D = 256
FB = D // P
IMGS, TOK = 16, 36
NT = IMGS * TOK
PATCH = 3 * 16 * 16
PK = PATCH // P
WARM = 9
WARM1 = 12
WARM2 = 18
WARM3 = 3
WARM4, WARM5, WARM6 = 8, 12, 6
PIECES = 3
CH = 2
CI = IMGS // CH
CT = NT // CH
TP = TOK + 1
HK = 1024 // P
FF = 768
FK = FF // P
EMB = 3
SQ1 = 5
POOLED = (4, 5)
POOLED2 = (3, 4, 5)
UP_EARLY = 2
QB = 32
NQB = FF * D // P // QB
LN_EPS = 1e-5
NEG = -1e38
RND = 1.5 * 2.0 ** 23
WTOP = 1024.0
QMAX = 32767.0
TINY = 1e-12

VECS = ["L0_tok_b", "L0_attn_ln1_w", "L0_attn_ln1_b", "L0_attn_ln2_w", "L0_attn_ln2_b", "L0_attn_att_tmk",
        "L0_attn_att_tmv", "L0_attn_att_tmr", "L0_attn_time_decay", "L0_attn_time_first", "L0_attn_ffn_tmk",
        "L0_attn_ffn_tmr"]


def build(nc, patches_d, vecs_d, wtok_d, wk_d, wv_d, wr_d, wo_d, wrec_d, wkey_d, wval_d, wgate_d, wup_d,
          wdown_d, out_d):
    fp32, fp16 = mybir.dt.float32, mybir.dt.float16
    int16, uint16 = mybir.dt.int16, mybir.dt.uint16
    ALU = mybir.AluOpType
    ACT = mybir.ActivationFunctionType
    AX = mybir.AxisListType

    ctx = ExitStack()
    with ctx:
        def sb(name, *shape, dtype=fp32):
            return ctx.enter_context(nc.sbuf_tensor(name, list(shape), dtype))

        def sem(name):
            return ctx.enter_context(nc.semaphore(name))

        front = sb("front", P, PK * (NT + D))
        patches = front[:, 0:PK * NT].rearrange("p (c k t) -> p c k t", c=CH, k=PK)
        wtok = front[:, PK * NT:PK * (NT + D)].rearrange("p (k n) -> p k n", k=PK)
        hidden = front[:, 0:HK * NT].rearrange("p (k t) -> p k t", t=NT)
        vecs = sb("vecs", P, len(VECS), FB)
        wk, wv, wr, wo, wrec = (sb(n, P, FB, D) for n in ("wk", "wv", "wr", "wo", "wrec"))
        wkey = sb("wkey", P, FB, HK * P)
        wval = sb("wval", P, HK, D)
        ffn_raw = sb("ffn_raw", P, 3, FF * D // P)
        ffn_hi = sb("ffn_hi", P, 3, FF * D // P, dtype=fp16)
        ffn_lo = sb("ffn_lo", P, 3, FF * D // P, dtype=fp16)
        wgate, wup, wdown = (tuple(t[:, i, :].rearrange("p (k n) -> p k n", k=k) for t in (ffn_hi, ffn_lo))
                             for i, k in enumerate((FB, FB, FK)))
        tok_b, ln1_w, ln1_b, ln2_w, ln2_b, tmk, tmv, tmr, decay, first, ftmk, ftmr = (
            vecs[:, i, :] for i in range(len(VECS)))

        ident = sb("ident", P, P)
        mean_w = sb("mean_w", P, P)
        eps1 = sb("eps1", P, 1)
        eps2 = sb("eps2", P, 1)
        wneg = sb("wneg", P, FB)
        wseg = sb("wseg", P, FB, CI, TP)
        bmax = sb("bmax", P, 3, NQB)
        binv = sb("binv", P, 3, NQB)
        wrow = sb("wrow", P, 3, FK)
        wrinv = sb("wrinv", P, 3, FK)

        h = sb("h", P, FB, NT)
        dev = sb("dev", P, FB, NT)
        sq = sb("sq", P, FB, NT)
        lnr = sb("lnr", P, CH, 2, CT)
        x0 = sb("x0", P, FB, NT)
        hn = sb("hn", P, FB, IMGS, TP)
        dm = sb("dm", P, FB, NT)
        xk, xv, xr = (sb(n, P, FB, NT) for n in ("xk", "xv", "xr"))
        PT = FB * IMGS * TP
        arena = sb("arena", P, 12 * PT)

        def padded(i, n=1):
            return arena[:, i * PT:(i + n) * PT].rearrange("p (b i t) -> p b i t", i=IMGS, t=TP)

        kp = padded(0)
        pp = padded(1)
        ex = [padded(2 + j) for j in range(4)]
        ex01, ex23 = padded(2, 2), padded(4, 2)
        ev = padded(6)
        aa, bb = padded(7), padded(8)

        def plain(i):
            return arena[:, i * PT:i * PT + FB * NT].rearrange("p (b t) -> p b t", t=NT)

        v = plain(9)
        z = plain(10)
        ea = plain(11)
        num, den = sq, dm
        tmp = sb("tmp", P, FB, NT)

        def big(i):
            return arena[:, i * FK * NT:(i + 1) * FK * NT].rearrange("p (k t) -> p k t", t=NT)

        gate, up, sig = big(0), big(1), big(2)

        def half(t, n, dtype):
            w = FK * NT // 2
            return t[:, n * w:(n + 1) * w].bitcast(dtype).rearrange("p (k t) -> p k t", t=NT)

        gate_q, sig_q = half(arena, 6, int16), half(arena, 7, uint16)
        up_q, silu_q = half(front, 0, int16), half(front, 1, int16)
        prod_q, prod_hi, prod_lo = half(arena, 6, int16), half(arena, 7, fp16), half(arena, 0, fp16)
        gate_f, sig_f = xk, xv
        up_f, silu_f = (tmp[:, 0, :], tmp[:, 1, :], dm[:, 0, :]), (xr[:, 0, :], xr[:, 1, :], dm[:, 1, :])
        x_q = sb("x_q", P, FB, NT, dtype=int16)
        x_hi = sb("x_hi", P, FB, NT, dtype=fp16)
        x_lo = sb("x_lo", P, FB, NT, dtype=fp16)
        mx = sb("mx", P, 5, FK)
        mx1 = sb("mx1", P, 5)
        top = sb("top", P, 5)
        sc = sb("sc", P, 5)
        isc = sb("isc", P, 5)
        fac = sb("fac", P, 5)
        raw = sb("raw", P, 5)
        unit = sb("unit", P, 5)
        out_sc = sb("out_sc", P, FB)
        ps = ctx.enter_context(nc.psum_tensor("ps", [P, 8, 512], fp32))

        names = (["in_patch0_%d" % j for j in range(PIECES)] + ["in_wtok%d" % j for j in range(PIECES)]
                 + ["in_patch1"] + ["in_" + n for n in (
            "vecs", "wk", "wv", "wr", "wo", "wrec", "wkey", "wval", "ffn0", "ffn1", "ffn2")] + ["stored"])
        dma = {n: sem(n) for n in names}
        zeroed, const_ready, ident_ready = sem("zeroed"), sem("const_ready"), sem("ident_ready")
        wneg_ready, wseg_ready = sem("wneg_ready"), sem("wseg_ready")
        bmax_ready, bscale_ready, binv_ready = sem("bmax_ready"), sem("bscale_ready"), sem("binv_ready")
        wdiv_ready, wround_ready, wq_ready = sem("wdiv_ready"), sem("wround_ready"), sem("wq_ready")
        wrow_ready, wrinv_ready, brel_ready = sem("wrow_ready"), sem("wrinv_ready"), sem("brel_ready")
        wt_done, wt_hi_ready, wt_lo_ready = sem("wt_done"), sem("wt_hi_ready"), sem("wt_lo_ready")
        (tok_done, mean_done, var_done, k_done, v_done, r_done, o_done, rec_done, key_done, val_done) = (
            sem(n) for n in ("tok_done", "mean_done", "var_done", "k_done", "v_done", "r_done", "o_done",
                             "rec_done", "key_done", "val_done"))
        gate_done, up_done, down_done = sem("gate_done"), sem("up_done"), sem("down_done")
        h_ready, dev_ready, sq_ready, ln_ready, rstd_ready = (
            sem(n) for n in ("h_ready", "dev_ready", "sq_ready", "ln_ready", "rstd_ready"))
        h_dve_ready, dev_half_ready, sq_half_ready, fold_ready = (
            sem(n) for n in ("h_dve_ready", "dev_half_ready", "sq_half_ready", "fold_ready"))
        norm_ready, x0_ready, hn_ready, dm_ready, mix_ready = (
            sem(n) for n in ("norm_ready", "x0_ready", "hn_ready", "dm_ready", "mix_ready"))
        kp_ready, v_ready, z_ready, abs_ready, ea_ready = (
            sem(n) for n in ("kp_ready", "v_ready", "z_ready", "abs_ready", "ea_ready"))
        pp_ready, arg01_ready, arg2_ready, arg3_ready, diff_ready, exp01_ready, exp23_ready = (
            sem(n) for n in ("pp_ready", "arg01_ready", "arg2_ready", "arg3_ready", "diff_ready", "exp01_ready", "exp23_ready"))
        num_ready, arg1_ready, relus_ready = sem("num_ready"), sem("arg1_ready"), sem("relus_ready")
        ev_ready, state_ready, n2_ready, part_ready, frac_ready = (
            sem(n) for n in ("ev_ready", "state_ready", "n2_ready", "part_ready", "frac_ready"))
        scaled_ready, lnden_ready, logq_ready, quot_ready, rw_ready = (
            sem(n) for n in ("scaled_ready", "lnden_ready", "logq_ready", "quot_ready", "rw_ready"))
        x1_ready, hx_ready, relu_ready, hid_ready, hid_dve_ready = (
            sem(n) for n in ("x1_ready", "hx_ready", "relu_ready", "hid_ready", "hid_dve_ready"))
        soft_ready, logsig_ready, recsig_ready, gated_ready, h2_ready = (
            sem(n) for n in ("soft_ready", "logsig_ready", "recsig_ready", "gated_ready", "h2_ready"))
        mx_ready, mx1_ready, mxb_done, top_ready, scale_step, fac_ready, scale_ready = (
            sem(n) for n in ("mx_ready", "mx1_ready", "mxb_done", "top_ready", "scale_step",
                             "fac_ready", "scale_ready"))
        gate_f_ready, sig_f_ready, up_f_ready, silu_f_ready, silu_pool_ready, prod_pool_ready = (
            sem(n) for n in ("gate_f_ready", "sig_f_ready", "up_f_ready", "silu_f_ready", "silu_pool_ready",
                             "prod_pool_ready"))
        mxup_ready, mxsilu_ready = sem("mxup_ready"), sem("mxsilu_ready")
        xq_ready, xhi_ready, xlo_ready = sem("xq_ready"), sem("xhi_ready"), sem("xlo_ready")
        gate_ready, up_ready = sem("gate_ready"), sem("up_ready")
        gq_ready, sig_ready, sigq_ready, silu_ready = (
            sem(n) for n in ("gq_ready", "sig_ready", "sigq_ready", "silu_ready"))
        gq0_ready, uq_pool_ready, up_f5_ready, tq_pool_ready, tq0_ready, oq0_ready = (
            sem(n) for n in ("gq0_ready", "uq_pool_ready", "up_f5_ready", "tq_pool_ready", "tq0_ready",
                             "oq0_ready"))
        tq_ready, uq_ready, prod_ready, oq_ready, ohi_ready, olo_ready, out_sc_ready, out_ready = (
            sem(n) for n in ("tq_ready", "uq_ready", "prod_ready", "oq_ready", "ohi_ready", "olo_ready",
                             "out_sc_ready", "out_ready"))

        def cols(t, c):
            return t[:, :, c * CT:(c + 1) * CT]

        def imgs(t, c, b=None):
            t = cols(t, c) if b is None else t[:, b, c * CT:(c + 1) * CT]
            return t.rearrange("p b (i t) -> p b i t" if b is None else "p (i t) -> p i t", t=TOK)

        def now(t, c, b=None):
            s = slice(c * CI, (c + 1) * CI)
            return t[:, :, s, 1:TP] if b is None else t[:, b, s, 1:TP]

        def before(t, c, b=None):
            s = slice(c * CI, (c + 1) * CI)
            return t[:, :, s, 0:TOK] if b is None else t[:, b, s, 0:TOK]

        def run(t, c, b):
            return t[:, b, c * CI:(c + 1) * CI, :].rearrange("p i t -> p (i t)")

        def bank(n, count=1):
            return ps[:, n, 0:CT] if count == 1 else ps[:, n:n + count, 0:CT]

        def bank_imgs(n):
            return ps[:, n:n + 2, 0:CT].rearrange("p b (i t) -> p b i t", t=TOK)

        def twice(ap):
            return ap.unsqueeze(1).to_broadcast([P, FB, CT])

        TOKB, MEAN1, VAR1 = (0, 2), (4, 5), (6, 7)
        KB, VB, RB = (0, 6), (2, 0), (4, 2)
        WTB = (0, 1, 4, 5, 0, 1, 0, 5, 4)
        OB, MEAN2, VAR2, RECB, KEYB, VALB = (4, 0), (6, 0), (7, 1), (4, 0), (2, 3), (6, 4)
        MEAN3, VAR3 = (6, 2), (7, 3)
        MEAN, VAR = (MEAN1, MEAN2, MEAN3), (VAR1, VAR2, VAR3)
        HALVED = ((0, 0), (1, 0), (2, 1))
        TILEB = (2, 3, 4, 5, 0, 1)
        MXB = 6
        block = ctx.enter_context(nc.Block())

        @block.sync
        def _(sp):
            for j in range(PIECES):
                s = slice(j * PK // PIECES, (j + 1) * PK // PIECES)
                sp.dma_start(wtok[:, s, :], wtok_d[:, s, :]).then_inc(dma["in_wtok%d" % j], 16)
                sp.dma_start(patches[:, 0, s, :], patches_d[:, 0, s, :]).then_inc(dma["in_patch0_%d" % j], 16)
            sp.dma_start(patches[:, 1, :, :], patches_d[:, 1, :, :]).then_inc(dma["in_patch1"], 16)
            sp.dma_start(wk[:, :, :], wk_d).then_inc(dma["in_wk"], 16)
            sp.dma_start(wv[:, :, :], wv_d).then_inc(dma["in_wv"], 16)
            sp.dma_start(wr[:, :, :], wr_d).then_inc(dma["in_wr"], 16)
            sp.dma_start(wo[:, :, :], wo_d).then_inc(dma["in_wo"], 16)
            sp.dma_start(wrec[:, :, :], wrec_d).then_inc(dma["in_wrec"], 16)
            sp.dma_start(wkey[:, :, :], wkey_d).then_inc(dma["in_wkey"], 16)
            sp.dma_start(wval[:, :, :], wval_d).then_inc(dma["in_wval"], 16)
            for i, w in enumerate((wgate_d, wup_d, wdown_d)):
                sp.dma_start(ffn_raw[:, i, :], w).then_inc(dma["in_ffn%d" % i], 16)
            for c in range(CH):
                for m in range(FB):
                    sp.wait_ge(out_ready, FB * c + m + 1)
                    sp.dma_start(out_d[:, m, c * CT:(c + 1) * CT], x0[:, m, c * CT:(c + 1) * CT])\
                        .then_inc(dma["stored"], 16)
            sp.wait_ge(dma["stored"], 16 * CH * FB)

        @block.gpsimd
        def _(pool):
            pool.memset(ident[:, :], 0.0).then_inc(zeroed, 1)
            pool.memset(mean_w[:, :], 1.0 / D).then_inc(const_ready, 1)
            pool.memset(eps1[:, :], LN_EPS).then_inc(const_ready, 1)
            pool.memset(eps2[:, :], LN_EPS * LN_EPS).then_inc(const_ready, 1)
            pool.wait_ge(zeroed, 1)
            pool.affine_select(out=ident[:, :], in_=ident[:, :], compare_op=ALU.not_equal, fill=1.0, base=0,
                               pattern=[[-1, P]], channel_multiplier=1).then_inc(ident_ready, 1)
            pool.memset(hn[:, :, :, 0:1], 0.0).then_inc(const_ready, 1)
            pool.memset(kp[:, :, :, 0:1], NEG).then_inc(const_ready, 1)
            for j in (0, 1):
                pool.memset(ex[j][:, :, :, 0:1], 0.0).then_inc(const_ready, 1)
            pool.memset(ev[:, :, :, 0:1], 0.0).then_inc(const_ready, 1)
            pool.memset(wseg[:, :, :, 0:1], NEG).then_inc(const_ready, 1)
            def divide(i):
                w3 = ffn_raw[:, i, :].rearrange("p (n q) -> p n q", q=QB)
                pool.wait_ge(binv_ready, i + 1)
                pool.tensor_tensor(w3, w3, binv[:, i, :].unsqueeze(2).to_broadcast([P, NQB, QB]),
                                   ALU.mult).then_inc(wdiv_ready, 1)

            def rescale(i):
                w3 = ffn_raw[:, i, :].rearrange("p (n q) -> p n q", q=QB)
                pool.wait_ge(wround_ready, i + 1)
                pool.wait_ge(brel_ready, i + 1)
                pool.tensor_tensor(w3, w3, bmax[:, i, :].unsqueeze(2).to_broadcast([P, NQB, QB]),
                                   ALU.mult).then_inc(wq_ready, 1)

            def bonus(c):
                pool.wait_ge(exp23_ready, c + 1)
                pool.wait_ge(v_ready, c + 1)
                pool.tensor_tensor(imgs(tmp, c), now(ex[3], c), imgs(v, c), ALU.mult).then_inc(n2_ready, 1)

            def outer_norm(c):
                pool.wait_ge(rstd_ready, c + 1)
                pool.tensor_tensor(cols(x0, c), cols(dev, c), twice(lnr[:, c, 0, :]), ALU.mult)\
                    .then_inc(x0_ready, 1)

            def inner_norm(c):
                pool.wait_ge(norm_ready, c)
                pool.wait_ge(rstd_ready, c + 1)
                pool.tensor_tensor(cols(tmp, c), cols(dev, c), twice(lnr[:, c, 1, :]), ALU.mult)\
                    .then_inc(norm_ready, 1)

            def arrival(c):
                pool.wait_ge(kp_ready, c + 1)
                pool.wait_ge(pp_ready, FB * (c + 1))
                pool.tensor_tensor(now(ex[1], c), now(kp, c), now(pp, c), ALU.subtract).then_inc(arg1_ready, 1)

            def bring(c):
                pool.wait_ge(exp01_ready, c + 1)
                pool.wait_ge(v_ready, c + 1)
                pool.tensor_tensor(now(ev, c), now(ex[1], c), imgs(v, c), ALU.mult).then_inc(ev_ready, 1)

            def numerator(c):
                pool.wait_ge(n2_ready, c + 1)
                pool.wait_ge(part_ready, 2 * c + 2)
                pool.tensor_tensor(cols(num, c), cols(num, c), cols(tmp, c), ALU.add).then_inc(num_ready, 1)

            outer_norm(0)
            arrival(0)
            inner_norm(1)
            bring(0)
            pool.wait_ge(hn_ready, FB * CH)
            pool.tensor_tensor(imgs(dm, 1), now(hn, 1), before(hn, 1), ALU.subtract).then_inc(dm_ready, 1)
            bonus(0)
            numerator(0)
            outer_norm(1)
            arrival(1)
            bring(1)
            divide(0)
            bonus(1)
            numerator(1)

            def hx(c):
                pool.wait_ge(x1_ready, FB * (c + 1))
                pool.tensor_tensor(cols(h, c), cols(h, c), cols(x0, c), ALU.add).then_inc(hx_ready, 1)

            def squares(c, ms):
                for m in ms:
                    pool.wait_ge(relu_ready, HK * c + m + 1)
                    t = hidden[:, m, c * CT:(c + 1) * CT]
                    pool.tensor_tensor(t, t, t, ALU.mult).then_inc(hid_ready, 1)

            hx(0)
            rescale(0)
            squares(0, range(0, 4, 2))
            divide(1)
            squares(0, range(4, HK, 2))
            rescale(1)
            hx(1)
            divide(2)
            squares(1, range(SQ1))
            rescale(2)

            def to_int(dst, src, i, m, ready):
                pool.wait_ge(fac_ready, i + 1)
                pool.tensor_scalar(dst[:, m, :], src[:, m, :], fac[:, i:i + 1], 0.0, ALU.mult, ALU.add)\
                    .then_inc(ready, 1)

            for m in range(FK + 1):
                if 1 <= m < FK:
                    to_int(gate_q, gate, 1, m, gq_ready)
                if m:
                    pool.wait_ge(sig_ready, m)
                    pool.tensor_scalar(sig_q[:, m - 1, :], sig[:, m - 1, :], 65536.0, 0.0, ALU.mult, ALU.add)\
                        .then_inc(sigq_ready, 1)
            for j, m in enumerate(POOLED):
                pool.wait_ge(gate_f_ready, j + 1)
                pool.wait_ge(sig_f_ready, j + 1)
                pool.tensor_tensor(sig[:, m, :], sig_f[:, j, :], gate_f[:, j, :], ALU.mult)\
                    .then_inc(silu_pool_ready, 1)
            for m in (5, 1, 2):
                to_int(up_q, up, 2, m, uq_pool_ready)
            to_int(silu_q, sig, 3, 1, tq_pool_ready)
            for j, m in enumerate(POOLED2):
                pool.wait_ge(silu_f_ready, j + 1)
                if m == 5:
                    pool.wait_ge(up_f5_ready, 1)
                else:
                    pool.wait_ge(up_f_ready, j + 1)
                pool.tensor_tensor(up[:, m, :], silu_f[j], up_f[j], ALU.mult).then_inc(prod_pool_ready, 1)

        @block.scalar
        def _(act):
            act.dma_start(vecs[:, :, :], vecs_d).then_inc(dma["in_vecs"], 16)
            act.preload_act_table_set("natural_log_exp_and_others")
            act.wait_ge(dma["in_vecs"], 16)
            act.activation(wneg[:, :], decay, ACT.Exp).then_inc(wneg_ready, 1)
            act.wait_ge(const_ready, 3)

            def embed(c, b):
                act.wait_ge(tok_done, FB * c + b + 1)
                act.activation(h[:, b, c * CT:(c + 1) * CT], bank(TOKB[c] + b), ACT.Identity,
                               bias=tok_b[:, b:b + 1]).then_inc(h_ready, 1)

            def square(n, c):
                s = slice(c * CT, (c + 1) * CT)
                if (n, c) in HALVED:
                    act.wait_ge(dev_half_ready, HALVED.index((n, c)) + 1)
                    act.activation(sq[:, 0, s], dev[:, 0, s], ACT.Square).then_inc(sq_half_ready, 1)
                    act.wait_ge(dev_ready, CH * n + c + 1)
                    act.activation(sq[:, 1, s], dev[:, 1, s], ACT.Square).then_inc(sq_ready, 1)
                else:
                    act.wait_ge(dev_ready, CH * n + c + 1)
                    act.activation(cols(sq, c), cols(dev, c), ACT.Square).then_inc(sq_ready, 1)

            def rstd(n, c):
                act.wait_ge(var_done, CH * n + c + 1)
                t = lnr[:, c, 0, :]
                act.activation(t, bank(VAR[n][c]), ACT.Ln, bias=eps1[:, :]).then_inc(ln_ready, 1)
                if n == 0:
                    act.activation(lnr[:, c, 1, :], bank(VAR[n][c]), ACT.Ln, bias=eps2[:, :],
                                   scale=1.0 + LN_EPS).then_inc(ln_ready, 1)
                    t = lnr[:, c, :, :]
                    act.wait_ge(ln_ready, 2 * (c + 1))
                else:
                    act.wait_ge(ln_ready, 2 * CH + CH * (n - 1) + c + 1)
                act.activation(t, t, ACT.Exp, scale=-0.5).then_inc(rstd_ready, 1)

            def key_out(c):
                act.wait_ge(k_done, c + 1)
                act.activation(now(kp, c), bank_imgs(KB[c]), ACT.Copy).then_inc(kp_ready, 1)

            def value_out(c):
                act.wait_ge(v_done, c + 1)
                act.activation(cols(v, c), bank(VB[c], 2), ACT.Copy).then_inc(v_ready, 1)

            def receptance_out(c):
                act.wait_ge(r_done, c + 1)
                act.activation(cols(ea, c), bank(RB[c], 2), ACT.Abs).then_inc(abs_ready, 1)
                act.wait_ge(abs_ready, c + 1)
                act.activation(cols(ea, c), cols(ea, c), ACT.Exp, scale=-1.0).then_inc(ea_ready, 1)
                act.activation(cols(z, c), bank(RB[c], 2), ACT.Copy).then_inc(z_ready, 1)

            def exps01(c):
                act.wait_ge(arg01_ready, FB * (c + 1))
                act.wait_ge(arg1_ready, c + 1)
                act.activation(now(ex01, c), now(ex01, c), ACT.Exp).then_inc(exp01_ready, 1)

            def exps23(c):
                if c == 1:
                    act.wait_ge(diff_ready, FB * (c + 1))
                    act.activation(now(ex[2], c), now(ex[3], c), ACT.Relu).then_inc(arg2_ready, 1)
                    act.wait_ge(arg2_ready, 1)
                    act.activation(now(ex[3], c), now(ex[3], c), ACT.Relu, scale=-1.0).then_inc(arg3_ready, 1)
                    act.wait_ge(arg3_ready, 1)
                else:
                    act.wait_ge(relus_ready, 2)
                act.activation(now(ex23, c), now(ex23, c), ACT.Exp, scale=-1.0).then_inc(exp23_ready, 1)

            def lnden(c):
                act.wait_ge(scaled_ready, c + 1)
                act.activation(cols(den, c), cols(den, c), ACT.Ln).then_inc(lnden_ready, 1)

            def quot(c):
                act.wait_ge(logq_ready, c + 1)
                act.activation(cols(den, c), cols(den, c), ACT.Exp).then_inc(quot_ready, 1)

            def weights_out(g0, g1):
                flat = ffn_hi[:, :, :].rearrange("p a b -> p (a b)")
                for g in range(g0, g1):
                    act.wait_ge(wt_done, g + 1)
                    act.activation(flat[:, g * 512:(g + 1) * 512], ps[:, WTB[g], :], ACT.Copy)\
                        .then_inc(wt_hi_ready, 1)

            def gate_out(c):
                act.wait_ge(rec_done, c + 1)
                act.wait_ge(logq_ready, c + 1)
                act.wait_ge(scaled_ready, c + 1)
                act.activation(cols(z, c), bank(RECB[c], 2), ACT.Copy).then_inc(z_ready, 1)
                act.activation(cols(ea, c), bank(RECB[c], 2), ACT.Abs).then_inc(abs_ready, 1)

            def soft(c):
                act.wait_ge(abs_ready, CH + c + 1)
                act.activation(cols(ea, c), cols(ea, c), ACT.Exp, scale=-1.0).then_inc(ea_ready, 1)

            def soft_log(c):
                act.wait_ge(ea_ready, CH + c + 1)
                act.activation(cols(ea, c), cols(ea, c), ACT.Ln, bias=1.0).then_inc(soft_ready, 1)

            def recsig(c):
                act.wait_ge(logsig_ready, c + 1)
                act.activation(cols(ea, c), cols(ea, c), ACT.Exp).then_inc(recsig_ready, 1)

            def relu(c, m):
                act.wait_ge(key_done, HK * c + m + 1)
                if c == 0 and m == 0:
                    act.wait_ge(tok_done, FB * CH)
                act.activation(hidden[:, m, c * CT:(c + 1) * CT], bank(KEYB[m % 2]), ACT.Relu)\
                    .then_inc(relu_ready, 1)

            embed(0, 0)
            square(0, 0)
            rstd(0, 0)
            embed(1, 0)
            embed(1, 1)
            square(0, 1)
            key_out(0)
            rstd(0, 1)
            value_out(0)
            exps01(0)
            exps23(0)
            receptance_out(0)
            lnden(0)
            key_out(1)
            quot(0)
            value_out(1)
            exps01(1)
            square(1, 0)
            rstd(1, 0)
            exps23(1)
            receptance_out(1)
            relu(0, 0)
            relu(0, 1)
            lnden(1)
            relu(0, 2)
            quot(1)
            relu(0, 3)
            gate_out(0)
            relu(0, 4)
            soft(0)
            relu(0, 5)
            soft_log(0)
            relu(0, 6)
            relu(0, 7)
            square(1, 1)
            rstd(1, 1)
            recsig(0)
            gate_out(1)
            relu(1, 0)
            relu(1, 1)
            soft(1)
            relu(1, 2)
            soft_log(1)
            relu(1, 3)
            recsig(1)
            square(2, 0)
            for m in range(4, HK):
                relu(1, m)
            rstd(2, 0)
            weights_out(0, 1)
            square(2, 1)
            weights_out(1, 3)
            rstd(2, 1)
            weights_out(3, 6)
            act.preload_act_table_set("sigmoid_and_others")

            def evacuate(dst, i, done, ready, m):
                for c in range(CH):
                    act.wait_ge(done, CH * m + c + 1)
                    act.activation(dst[:, m, c * CT:(c + 1) * CT], bank(TILEB[(CH * m + c) % 6]), ACT.Copy,
                                   scale=wrow[:, i, m:m + 1]).then_inc(ready, 1)

            def to_int(dst, src, i, m, ready):
                act.activation(dst[:, m, :], src[:, m, :], ACT.Copy, scale=fac[:, i:i + 1]).then_inc(ready, 1)

            act.wait_ge(wrow_ready, 3 * 2)
            for m in range(FK):
                evacuate(gate, 0, gate_done, gate_ready, m)
            for m in range(2):
                evacuate(up, 1, up_done, up_ready, m)
            act.wait_ge(scale_ready, 2)
            for m in range(FK):
                if m == 0:
                    act.wait_ge(gq0_ready, 1)
                else:
                    act.wait_ge(gq_ready, m)
                act.activation(sig[:, m, :], gate_q[:, m, :], ACT.Sigmoid, scale=sc[:, 1:2])\
                    .then_inc(sig_ready, 1)
                if m + 2 < FK:
                    evacuate(up, 1, up_done, up_ready, m + 2)
            for j, m in enumerate(POOLED):
                act.wait_ge(gq_ready, m)
                act.activation(gate_f[:, j, :], gate_q[:, m, :], ACT.Copy).then_inc(gate_f_ready, 1)
                act.wait_ge(sigq_ready, m + 1)
                act.activation(sig_f[:, j, :], sig_q[:, m, :], ACT.Copy).then_inc(sig_f_ready, 1)
            act.wait_ge(fac_ready, 3)
            for j, m in enumerate((3, 4)):
                to_int(up_q, up, 2, m, uq_ready)
                act.wait_ge(uq_ready, j + 1)
                act.activation(up_f[j], up_q[:, m, :], ACT.Copy).then_inc(up_f_ready, 1)
            to_int(up_q, up, 2, 0, uq_ready)
            act.wait_ge(fac_ready, 4)
            for m in (3, 2, 4, 5):
                to_int(silu_q, sig, 3, m, tq_ready)
                if m in POOLED2:
                    act.wait_ge(tq_ready, (3, 2, 4, 5).index(m) + 1)
                    act.activation(silu_f[m - POOLED2[0]], silu_q[:, m, :], ACT.Copy).then_inc(silu_f_ready, 1)
            weights_out(6, 9)
            act.wait_ge(fac_ready, 5)
            for m in range(1, FK):
                to_int(prod_q, up, 4, m, oq_ready)

        @block.vector
        def _(dve):
            def round_weights(i):
                dve.wait_ge(dma["in_ffn%d" % i], 16)
                w3 = ffn_raw[:, i, :].rearrange("p (n q) -> p n q", q=QB)
                dve.tensor_reduce(bmax[:, i, :], w3, AX.X, ALU.max, apply_absolute_value=True)\
                    .then_inc(bmax_ready, 1)
                dve.wait_ge(bmax_ready, i + 1)
                dve.tensor_scalar(bmax[:, i, :], bmax[:, i, :], 1.0 / 7.0, TINY, ALU.mult, ALU.max)\
                    .then_inc(bscale_ready, 1)
                dve.wait_ge(bscale_ready, i + 1)
                dve.reciprocal(binv[:, i, :], bmax[:, i, :]).then_inc(binv_ready, 1)

            def row_scales(i):
                blocks = FK if i < 2 else FB
                s3 = bmax[:, i, :].rearrange("p (m n) -> p m n", m=blocks)
                dve.tensor_reduce(wrow[:, i, 0:blocks], s3, AX.X, ALU.max).then_inc(wrow_ready, 1)
                dve.wait_ge(wrow_ready, 2 * i + 1)
                dve.reciprocal(wrinv[:, i, 0:blocks], wrow[:, i, 0:blocks]).then_inc(wrinv_ready, 1)
                dve.wait_ge(wrinv_ready, i + 1)
                dve.scalar_tensor_tensor(s3, s3, WTOP, wrinv[:, i, 0:blocks].unsqueeze(2)
                                         .to_broadcast([P, blocks, NQB // blocks]), ALU.mult, ALU.mult)\
                    .then_inc(brel_ready, 1)
                dve.tensor_scalar(wrow[:, i, 0:blocks], wrow[:, i, 0:blocks], 1.0 / WTOP, None, ALU.mult)\
                    .then_inc(wrow_ready, 1)

            def weights_low(g0, g1):
                flat, low = (t[:, :, :].rearrange("p a b -> p (a b)") for t in (ffn_hi, ffn_lo))
                for g in range(g0, g1):
                    s = slice(g * 512, (g + 1) * 512)
                    dve.wait_ge(wt_hi_ready, g + 1)
                    dve.tensor_tensor(low[:, s], ps[:, WTB[g], :], flat[:, s], ALU.subtract)\
                        .then_inc(wt_lo_ready, 1)

            def round_weights2(i):
                dve.wait_ge(wdiv_ready, i + 1)
                dve.tensor_scalar(ffn_raw[:, i, :], ffn_raw[:, i, :], RND, RND, ALU.add, ALU.subtract)\
                    .then_inc(wround_ready, 1)

            def embed(c, b):
                dve.wait_ge(dma["in_vecs"], 16)
                dve.wait_ge(tok_done, FB * c + b + 1)
                dve.tensor_scalar(h[:, b, c * CT:(c + 1) * CT], bank(TOKB[c] + b), tok_b[:, b:b + 1], None,
                                  ALU.add).then_inc(h_dve_ready, 1)

            def deviation(n, c):
                src = x0 if n == 1 else h
                dve.wait_ge(mean_done, CH * n + c + 1)
                if (n, c) in HALVED:
                    s = slice(c * CT, (c + 1) * CT)
                    dve.tensor_tensor(dev[:, 0, s], src[:, 0, s], bank(MEAN[n][c]), ALU.subtract)\
                        .then_inc(dev_half_ready, 1)
                    dve.tensor_tensor(dev[:, 1, s], src[:, 1, s], bank(MEAN[n][c]), ALU.subtract)\
                        .then_inc(dev_ready, 1)
                else:
                    dve.tensor_tensor(cols(dev, c), cols(src, c), twice(bank(MEAN[n][c])), ALU.subtract)\
                        .then_inc(dev_ready, 1)

            def fold_tokens(n, c):
                src = x0 if n == 1 else h
                s = slice(c * CT, (c + 1) * CT)
                if n == 1:
                    dve.wait_ge(x1_ready, FB * (c + 1))
                else:
                    dve.wait_ge(h2_ready, FB * (c + 1))
                dve.tensor_tensor(dev[:, 0, s], src[:, 0, s], src[:, 1, s], ALU.add).then_inc(fold_ready, 1)

            def fold_squares(n, c):
                s = slice(c * CT, (c + 1) * CT)
                dve.wait_ge(sq_ready, CH * n + c + 1)
                dve.tensor_tensor(sq[:, 0, s], sq[:, 0, s], sq[:, 1, s], ALU.add).then_inc(fold_ready, 1)

            def normalise(n, c):
                dve.wait_ge(rstd_ready, CH * n + c + 1)
                dst = tmp if n == 0 else dev
                dve.tensor_tensor(cols(dst, c), cols(dev, c), twice(lnr[:, c, 1 if n == 0 else 0, :]), ALU.mult)\
                    .then_inc(norm_ready, 1)

            def affine(n, c):
                dve.wait_ge(norm_ready, CH * n + c + 1)
                for b in range(FB):
                    w, o = ((ln1_w, ln1_b), (ln2_w, ln2_b))[n]
                    dve.tensor_scalar(now(hn, c, b), imgs(tmp if n == 0 else dev, c, b), w[:, b:b + 1], o[:, b:b + 1],
                                      ALU.mult, ALU.add).then_inc(hn_ready, 1)

            def shift(n, c):
                dve.wait_ge(hn_ready, FB * (CH * n + c + 1))
                if n == 1:
                    dve.wait_ge(rw_ready, c + 1)
                dve.tensor_tensor(imgs(dm, c), now(hn, c), before(hn, c), ALU.subtract).then_inc(dm_ready, 1)

            def mix(n, c, j):
                dve.wait_ge(dm_ready, CH * n + c + 1)
                dst, m = (((xk, tmk), (xv, tmv), (xr, tmr)) if n == 0 else ((xr, ftmr), (xk, ftmk)))[j]
                for b in range(FB):
                    dve.scalar_tensor_tensor(imgs(dst, c, b), imgs(dm, c, b), m[:, b:b + 1],
                                             before(hn, c, b), ALU.mult, ALU.add).then_inc(mix_ready, 1)

            def maxima(c):
                dve.wait_ge(kp_ready, c + 1)
                for b in range(FB):
                    dve.tensor_tensor_scan(run(pp, c, b), wseg[:, b, :, :].rearrange("p i t -> p (i t)"),
                                           run(kp, c, b), NEG, ALU.add, ALU.max).then_inc(pp_ready, 1)

            def exponents(c):
                dve.wait_ge(pp_ready, FB * (c + 1))
                for b in range(FB):
                    dve.scalar_tensor_tensor(now(ex[0], c, b), before(pp, c, b), wneg[:, b:b + 1],
                                             now(pp, c, b), ALU.add, ALU.subtract).then_inc(arg01_ready, 1)

            def bonus_exponents(c):
                for b in range(FB):
                    dve.scalar_tensor_tensor(now(ex[3], c, b), now(kp, c, b), first[:, b:b + 1],
                                             before(pp, c, b), ALU.add, ALU.subtract).then_inc(diff_ready, 1)

            def relus():
                dve.wait_ge(diff_ready, FB)
                dve.tensor_scalar(now(ex[2], 0), now(ex[3], 0), 0.0, None, ALU.max).then_inc(relus_ready, 1)
                dve.wait_ge(relus_ready, 1)
                dve.tensor_scalar(now(ex[3], 0), now(ex[3], 0), -1.0, 0.0, ALU.mult, ALU.max)\
                    .then_inc(relus_ready, 1)

            def weight_state(c):
                dve.wait_ge(exp01_ready, c + 1)
                for b in range(FB):
                    dve.tensor_tensor_scan(run(bb, c, b), run(ex[0], c, b), run(ex[1], c, b), 0.0,
                                           ALU.mult, ALU.add).then_inc(state_ready, 1)

            def value_state(c):
                dve.wait_ge(ev_ready, c + 1)
                for b in range(FB):
                    dve.tensor_tensor_scan(run(aa, c, b), run(ex[0], c, b), run(ev, c, b), 0.0,
                                           ALU.mult, ALU.add).then_inc(state_ready, 1)

            def weight_part(c):
                dve.wait_ge(exp23_ready, c + 1)
                dve.wait_ge(state_ready, 2 * FB * c + FB)
                dve.tensor_tensor(imgs(den, c), now(ex[2], c), before(bb, c), ALU.mult).then_inc(part_ready, 1)

            def value_part(c):
                dve.wait_ge(state_ready, 2 * FB * (c + 1))
                dve.tensor_tensor(imgs(num, c), now(ex[2], c), before(aa, c), ALU.mult).then_inc(part_ready, 1)

            def fraction(c):
                dve.wait_ge(part_ready, 2 * c + 1)
                dve.tensor_tensor(imgs(den, c), imgs(den, c), now(ex[3], c), ALU.add).then_inc(frac_ready, 1)
                dve.wait_ge(frac_ready, c + 1)
                dve.wait_ge(ea_ready, c + 1)
                dve.scalar_tensor_tensor(cols(den, c), cols(ea, c), 1.0, cols(den, c), ALU.add, ALU.mult)\
                    .then_inc(scaled_ready, 1)

            def logq(c):
                dve.wait_ge(lnden_ready, c + 1)
                dve.wait_ge(z_ready, c + 1)
                dve.scalar_tensor_tensor(cols(den, c), cols(z, c), 0.0, cols(den, c), ALU.min, ALU.subtract)\
                    .then_inc(logq_ready, 1)

            def rwkv(c):
                dve.wait_ge(quot_ready, c + 1)
                dve.wait_ge(num_ready, c + 1)
                dve.tensor_tensor(cols(xk, c), cols(num, c), cols(den, c), ALU.mult).then_inc(rw_ready, 1)

            def residual(c):
                dve.wait_ge(x0_ready, c + 1)
                s = slice(c * CT, (c + 1) * CT)
                for b in range(FB):
                    dve.wait_ge(o_done, FB * c + b + 1)
                    dve.tensor_tensor(x0[:, b, s], x0[:, b, s], bank(OB[c] + b), ALU.add).then_inc(x1_ready, 1)

            def square_relu(c, m):
                dve.wait_ge(relu_ready, HK * c + m + 1)
                t = hidden[:, m, c * CT:(c + 1) * CT]
                dve.tensor_tensor(t, t, t, ALU.mult).then_inc(hid_dve_ready, 1)

            def logsig(c):
                dve.wait_ge(soft_ready, c + 1)
                dve.scalar_tensor_tensor(cols(ea, c), cols(z, c), 0.0, cols(ea, c), ALU.min, ALU.subtract)\
                    .then_inc(logsig_ready, 1)

            def channel_out(c):
                dve.wait_ge(recsig_ready, c + 1)
                dve.wait_ge(hx_ready, c + 1)
                s = slice(c * CT, (c + 1) * CT)
                for b in range(FB):
                    dve.wait_ge(val_done, FB * c + b + 1)
                    dve.tensor_tensor(xv[:, b, s], ea[:, b, s], bank(VALB[c] + b), ALU.mult)\
                        .then_inc(gated_ready, 1)
                    dve.wait_ge(gated_ready, FB * c + b + 1)
                    dve.tensor_tensor(h[:, b, s], h[:, b, s], xv[:, b, s], ALU.add).then_inc(h2_ready, 1)

            dve.wait_ge(wneg_ready, 1)
            dve.tensor_scalar(wneg[:, :], wneg[:, :], -1.0, None, ALU.mult).then_inc(wneg_ready, 1)
            dve.wait_ge(wneg_ready, 2)
            dve.memset(wseg[:, :, :, 1:TP], 0.0).then_inc(wseg_ready, 1)
            dve.wait_ge(wseg_ready, 1)
            for b in range(FB):
                dve.tensor_scalar(wseg[:, b, :, 1:TP], wseg[:, b, :, 1:TP], wneg[:, b:b + 1], None, ALU.add)\
                    .then_inc(wseg_ready, 1)
            dve.wait_ge(wseg_ready, 1 + FB)
            embed(0, 1)
            deviation(0, 0)
            normalise(0, 0)
            dve.wait_ge(const_ready, 9)
            affine(0, 0)
            shift(0, 0)
            mix(0, 0, 0)
            deviation(0, 1)
            mix(0, 0, 1)
            mix(0, 0, 2)
            maxima(0)
            exponents(0)
            bonus_exponents(0)
            relus()
            affine(0, 1)
            weight_state(0)
            weight_part(0)
            value_state(0)
            mix(0, 1, 0)
            value_part(0)
            fraction(0)
            mix(0, 1, 1)
            logq(0)
            mix(0, 1, 2)
            rwkv(0)
            maxima(1)
            exponents(1)
            residual(0)
            bonus_exponents(1)
            deviation(1, 0)
            round_weights(0)
            normalise(1, 0)
            affine(1, 0)
            shift(1, 0)
            mix(1, 0, 0)
            mix(1, 0, 1)
            weight_state(1)
            value_state(1)
            weight_part(1)
            value_part(1)
            fraction(1)
            row_scales(0)
            logq(1)
            round_weights2(0)
            rwkv(1)
            square_relu(0, 1)
            square_relu(0, 3)
            round_weights(1)
            residual(1)
            fold_tokens(1, 1)
            logsig(0)
            row_scales(1)
            deviation(1, 1)
            square_relu(0, 5)
            fold_squares(1, 1)
            square_relu(0, 7)
            round_weights2(1)
            normalise(1, 1)
            affine(1, 1)
            shift(1, 1)
            mix(1, 1, 0)
            mix(1, 1, 1)
            channel_out(0)
            fold_tokens(2, 0)
            round_weights(2)
            row_scales(2)
            logsig(1)
            deviation(2, 0)
            fold_squares(2, 0)
            round_weights2(2)
            for m in range(SQ1, HK):
                square_relu(1, m)
            normalise(2, 0)
            dve.wait_ge(norm_ready, 2 * CH + 1)
            dve.tensor_reduce(mx[:, 0, 0:1], cols(dev, 0), AX.XY, ALU.max, apply_absolute_value=True)\
                .then_inc(mx_ready, 1)
            channel_out(1)
            deviation(2, 1)
            weights_low(0, 3)
            normalise(2, 1)
            dve.wait_ge(norm_ready, 2 * CH + 2)
            dve.tensor_reduce(mx[:, 0, 1:2], cols(dev, 1), AX.XY, ALU.max, apply_absolute_value=True)\
                .then_inc(mx_ready, 1)

            def reduce_max(i, count, ready, seen):
                dve.wait_ge(ready, seen)
                dve.tensor_reduce(mx1[:, i:i + 1], mx[:, i, 0:count], AX.X, ALU.max).then_inc(mx1_ready, 1)

            def core_max(i):
                dve.wait_ge(mxb_done, i + 1)
                dve.tensor_reduce(top[:, i:i + 1], ps[:, MXB, 0:P], AX.X, ALU.max).then_inc(top_ready, 1)

            steps = [0]

            def small(ins):
                steps[0] += 1
                ins.then_inc(scale_step, 1)
                dve.wait_ge(scale_step, steps[0])

            def scale(i, one):
                dve.wait_ge(top_ready, i + 1)
                small(dve.tensor_scalar(isc[:, i:i + 1], top[:, i:i + 1], 1.0 / QMAX, TINY if one is None else one[1],
                                        ALU.mult, ALU.max))
                dve.reciprocal(fac[:, i:i + 1], isc[:, i:i + 1]).then_inc(fac_ready, 1)
                dve.tensor_scalar(sc[:, i:i + 1], isc[:, i:i + 1], 1.0 if one is None else one[0], None, ALU.mult)\
                    .then_inc(scale_ready, 1)

            def worth(i, a, b):
                small(dve.tensor_scalar(raw[:, i:i + 1], a, b, None, ALU.mult))
                small(dve.reciprocal(unit[:, i:i + 1], raw[:, i:i + 1]))
                small(dve.tensor_scalar(unit[:, i:i + 1], unit[:, i:i + 1], TINY, None, ALU.mult))
                return raw[:, i:i + 1], unit[:, i:i + 1]

            reduce_max(0, CH, mx_ready, CH)
            weights_low(3, 4)
            core_max(0)
            scale(0, None)
            dve.wait_ge(fac_ready, 1)
            for c in range(CH):
                dve.tensor_scalar(cols(x_q, c), cols(dev, c), fac[:, 0:1], None, ALU.mult).then_inc(xq_ready, 1)
                dve.wait_ge(xq_ready, c + 1)
                dve.tensor_copy(cols(x_hi, c), cols(x_q, c)).then_inc(xhi_ready, 1)
                dve.wait_ge(xhi_ready, c + 1)
                dve.tensor_tensor(cols(x_lo, c), cols(x_q, c), cols(x_hi, c), ALU.subtract).then_inc(xlo_ready, 1)
            weights_low(4, 6)
            dve.wait_ge(scale_ready, 1)
            by_x = worth(1, sc[:, 0:1], 1.0)
            for m in range(FK):
                dve.wait_ge(gate_ready, CH * (m + 1))
                dve.tensor_reduce(mx[:, 1, m:m + 1], gate[:, m, :], AX.X, ALU.max, apply_absolute_value=True)\
                    .then_inc(mx_ready, 1)
            def up_max(m):
                dve.wait_ge(up_ready, CH * (m + 1))
                dve.tensor_reduce(mx[:, 2, m:m + 1], up[:, m, :], AX.X, ALU.max, apply_absolute_value=True)\
                    .then_inc(mxup_ready, 1)

            reduce_max(1, FK, mx_ready, CH + FK)
            core_max(1)
            up_max(0)
            scale(1, by_x)
            dve.wait_ge(fac_ready, 2)
            dve.tensor_scalar(gate_q[:, 0, :], gate[:, 0, :], fac[:, 1:2], None, ALU.mult).then_inc(gq0_ready, 1)
            up_max(1)
            dve.wait_ge(scale_ready, 2)
            by_silu = worth(3, sc[:, 1:2], 1.0 / 65536.0)
            for m in range(FK + 1):
                if m < POOLED[0]:
                    dve.wait_ge(sigq_ready, m + 1)
                    if m == 0:
                        dve.wait_ge(gq0_ready, 1)
                    else:
                        dve.wait_ge(gq_ready, m)
                    dve.tensor_tensor(sig[:, m, :], sig_q[:, m, :], gate_q[:, m, :], ALU.mult)\
                        .then_inc(silu_ready, 1)
                if m + 2 < FK:
                    up_max(m + 2)
                if m == 3:
                    reduce_max(2, FK, mxup_ready, FK)
                if m:
                    if m - 1 in POOLED:
                        dve.wait_ge(silu_pool_ready, m - POOLED[0])
                    else:
                        dve.wait_ge(silu_ready, m)
                    dve.tensor_reduce(mx[:, 3, m - 1:m], sig[:, m - 1, :], AX.X, ALU.max,
                                      apply_absolute_value=True).then_inc(mxsilu_ready, 1)
                if m == 3:
                    core_max(2)
                if m == 4:
                    scale(2, by_x)
            reduce_max(3, FK, mxsilu_ready, FK)
            dve.wait_ge(uq_pool_ready, 1)
            dve.tensor_copy(up_f[2], up_q[:, 5, :]).then_inc(up_f5_ready, 1)
            core_max(3)
            scale(3, by_silu)

            def product_max(m):
                if m in POOLED2:
                    dve.wait_ge(prod_pool_ready, m - POOLED2[0] + 1)
                else:
                    dve.wait_ge(prod_ready, m + 1)
                dve.tensor_reduce(mx[:, 4, m:m + 1], up[:, m, :], AX.X, ALU.max,
                                  apply_absolute_value=True).then_inc(mx_ready, 1)

            def up_product(m):
                dve.tensor_tensor(up[:, m, :], silu_q[:, m, :], up_q[:, m, :], ALU.mult).then_inc(prod_ready, 1)

            dve.wait_ge(fac_ready, 4)
            dve.tensor_scalar(silu_q[:, 0, :], sig[:, 0, :], fac[:, 3:4], None, ALU.mult).then_inc(tq0_ready, 1)
            dve.wait_ge(uq_ready, 3)
            dve.wait_ge(tq0_ready, 1)
            up_product(0)
            dve.wait_ge(scale_ready, 4)
            by_prod = worth(4, sc[:, 2:3], sc[:, 3:4])
            dve.wait_ge(uq_pool_ready, 2)
            dve.wait_ge(tq_pool_ready, 1)
            up_product(1)
            product_max(0)
            dve.wait_ge(uq_pool_ready, 3)
            dve.wait_ge(tq_ready, 2)
            up_product(2)
            for m in range(1, FK):
                product_max(m)
            reduce_max(4, FK, mx_ready, CH + 2 * FK)
            weights_low(6, 7)
            core_max(4)
            scale(4, by_prod)
            dve.wait_ge(fac_ready, 5)
            dve.tensor_scalar(prod_q[:, 0, :], up[:, 0, :], fac[:, 4:5], None, ALU.mult).then_inc(oq0_ready, 1)
            for m in range(FK):
                if m == 0:
                    dve.wait_ge(oq0_ready, 1)
                else:
                    dve.wait_ge(oq_ready, m)
                dve.tensor_copy(prod_hi[:, m, :], prod_q[:, m, :]).then_inc(ohi_ready, 1)
                dve.wait_ge(ohi_ready, m + 1)
                dve.tensor_tensor(prod_lo[:, m, :], prod_q[:, m, :], prod_hi[:, m, :], ALU.subtract)\
                    .then_inc(olo_ready, 1)
                if m == 2:
                    dve.wait_ge(scale_ready, 5)
                    dve.tensor_scalar(out_sc[:, :], wrow[:, 2, 0:FB], sc[:, 4:5], None, ALU.mult)\
                        .then_inc(out_sc_ready, 1)
                if m in (1, 3):
                    weights_low(7 + m // 2, 8 + m // 2)
            dve.wait_ge(out_sc_ready, 1)
            for c in range(CH):
                for m in range(FB):
                    dve.wait_ge(down_done, FB * c + m + 1)
                    s = slice(c * CT, (c + 1) * CT)
                    dve.scalar_tensor_tensor(x0[:, m, s], bank(FB * c + m), out_sc[:, m:m + 1], h[:, m, s],
                                             ALU.mult, ALU.add).then_inc(out_ready, 1)

        @block.tensor
        def _(pe):
            def product(dst, w, src, m, c, blocks, rhs=None):
                for k in range(blocks):
                    r = src[:, k, c * CT:(c + 1) * CT] if rhs is None else rhs(k)
                    last = pe.matmul(dst, w[:, k, m * P:(m + 1) * P], r, start=(k == 0), stop=(k == blocks - 1))
                return last

            def embed_first():
                for k in range(PK):
                    if k * PIECES % PK == 0:
                        pe.wait_ge(dma["in_wtok%d" % (k * PIECES // PK)], 16)
                        pe.wait_ge(dma["in_patch0_%d" % (k * PIECES // PK)], 16)
                    for m in range(FB):
                        last = pe.matmul(bank(TOKB[0] + m), wtok[:, k, m * P:(m + 1) * P], patches[:, 0, k, :],
                                         start=(k == 0), stop=(k == PK - 1))
                        if k == PK - 1:
                            last.then_inc(tok_done, 1)

            def embed(c, m, k0, k1):
                if (c, m, k0) == (1, 0, 0):
                    pe.wait_ge(dma["in_patch1"], 16)
                for k in range(k0, k1):
                    last = pe.matmul(bank(TOKB[c] + m), wtok[:, k, m * P:(m + 1) * P], patches[:, c, k, :],
                                     start=(k == 0), stop=(k == PK - 1))
                if k1 == PK:
                    last.then_inc(tok_done, 1)

            def spread(dst, src, c):
                for k in range(FB):
                    last = pe.matmul(dst, mean_w[:, :], src[:, k, c * CT:(c + 1) * CT], start=(k == 0),
                                     stop=(k == FB - 1))
                return last

            def project(w, src, banks, done, c):
                for m in range(FB):
                    last = product(bank(banks[c] + m), w, src, m, c, FB)
                last.then_inc(done, 1)

            def key_head(c):
                if c == 0:
                    pe.wait_ge(dma["in_wk"], 16)
                    pe.wait_ge(h_ready, FB * CH - 1)
                    pe.wait_ge(h_dve_ready, 1)
                else:
                    pe.wait_ge(ln_ready, 2 * CH)
                pe.wait_ge(mix_ready, 3 * FB * c + FB)
                project(wk, xk, KB, k_done, c)

            def value_head(c):
                if c == 0:
                    pe.wait_ge(dma["in_wv"], 16)
                else:
                    pe.wait_ge(kp_ready, 1)
                pe.wait_ge(mix_ready, 3 * FB * c + 2 * FB)
                project(wv, xv, VB, v_done, c)

            def receptance_head(c, m):
                if c == 0:
                    pe.wait_ge(dma["in_wr"], 16)
                    pe.wait_ge(dev_ready, CH)
                else:
                    pe.wait_ge(v_ready, 1)
                pe.wait_ge(mix_ready, 3 * FB * (c + 1))
                last = product(bank(RB[c] + m), wr, xr, m, c, FB)
                if m == FB - 1:
                    last.then_inc(r_done, 1)

            def weights(g0, g1):
                for g in range(g0, g1):
                    i = g // 3
                    pe.wait_ge(wq_ready, i + 1)
                    if g == 0:
                        pe.wait_ge(ident_ready, 1)
                        pe.wait_ge(z_ready, 2 * CH)
                        pe.wait_ge(abs_ready, 2 * CH)
                    if g in (4, 5):
                        pe.wait_ge(wt_lo_ready, g - 3)
                    kb, mb = (FB, FK) if i < 2 else (FK, FB)
                    for j in range(4):
                        k, m = divmod(4 * (g % 3) + j, mb)
                        last = pe.transpose(ps[:, WTB[g], j * P:(j + 1) * P],
                                            ffn_raw[:, i, (m * kb + k) * P:(m * kb + k + 1) * P], ident[:, :])
                    last.then_inc(wt_done, 1)

            def wkv_out(c):
                if c == 0:
                    pe.wait_ge(dma["in_wo"], 16)
                    pe.wait_ge(z_ready, 1)
                    pe.wait_ge(abs_ready, 1)
                else:
                    pe.wait_ge(v_ready, CH)
                pe.wait_ge(rw_ready, c + 1)
                for m in range(FB):
                    product(bank(OB[c] + m), wo, xk, m, c, FB).then_inc(o_done, 1)

            def warm(count, b):
                for _ in range(count):
                    pe.matmul(ps[:, b, 0:P], mean_w[:, :], mean_w[:, :], start=True, stop=True)

            def half_mean(dst, src, c, b):
                return pe.matmul(dst, mean_w[:, :], src[:, b, c * CT:(c + 1) * CT], start=(b == 0),
                                 stop=(b == FB - 1))

            def half_var(n, c):
                pe.wait_ge(sq_half_ready, HALVED.index((n, c)) + 1)
                half_mean(bank(VAR[n][c]), sq, c, 0)
                pe.wait_ge(sq_ready, CH * n + c + 1)
                half_mean(bank(VAR[n][c]), sq, c, 1).then_inc(var_done, 1)

            def mean1(c):
                pe.wait_ge(h_ready, FB * c + 1)
                if c == 0:
                    half_mean(bank(MEAN1[0]), h, 0, 0)
                    pe.wait_ge(h_dve_ready, 1)
                    half_mean(bank(MEAN1[0]), h, 0, 1).then_inc(mean_done, 1)
                else:
                    spread(bank(MEAN1[c]), h, c).then_inc(mean_done, 1)

            def var1():
                pe.wait_ge(sq_ready, 2)
                spread(bank(VAR1[1]), sq, 1).then_inc(var_done, 1)

            pe.wait_ge(const_ready, 1)
            warm(WARM, 7)
            embed_first()
            mean1(0)
            embed(1, 0, 0, EMB)
            half_var(0, 0)
            embed(1, 0, EMB, PK)
            embed(1, 1, 0, PK)
            mean1(1)
            key_head(0)
            var1()
            value_head(0)
            receptance_head(0, 0)
            receptance_head(0, 1)
            pe.wait_ge(ln_ready, 2)
            warm(WARM1, 6)
            key_head(1)
            value_head(1)
            wkv_out(0)
            def spread_fold(dst, src, c, count):
                pe.wait_ge(fold_ready, count)
                return pe.matmul(dst, mean_w[:, :], src[:, 0, c * CT:(c + 1) * CT], start=True, stop=True)

            def mean2(c):
                if c == 0:
                    pe.wait_ge(kp_ready, CH)
                    for b in range(FB):
                        pe.wait_ge(x1_ready, b + 1)
                        last = half_mean(bank(MEAN2[0]), x0, 0, b)
                    last.then_inc(mean_done, 1)
                else:
                    pe.wait_ge(x1_ready, FB * CH)
                    spread_fold(bank(MEAN2[c]), dev, c, 1).then_inc(mean_done, 1)

            def receptance(c):
                if c == 0:
                    pe.wait_ge(dma["in_wrec"], 16)
                else:
                    pe.wait_ge(dev_ready, CH + 2)
                    pe.wait_ge(ln_ready, 3 * CH)
                pe.wait_ge(mix_ready, 3 * FB * CH + 2 * FB * c + FB)
                project(wrec, xr, RECB, rec_done, c)

            def keys(c, m0, m1):
                if (c, m0) == (0, 0):
                    pe.wait_ge(dma["in_wkey"], 16)
                    pe.wait_ge(z_ready, CH)
                    pe.wait_ge(abs_ready, CH)
                pe.wait_ge(mix_ready, 3 * FB * CH + 2 * FB * (c + 1))
                for m in range(m0, m1):
                    n = HK * c + m
                    if n >= 2:
                        pe.wait_ge(relu_ready, n - 1)
                    product(bank(KEYB[m % 2]), wkey, xk, m, c, FB).then_inc(key_done, 1)

            def values(c, m, k0=0, k1=HK):
                if c == 0:
                    pe.wait_ge(dma["in_wval"], 16)
                    pe.wait_ge(dev_ready, CH + 1)
                    pe.wait_ge(ln_ready, 2 * CH + 1)
                else:
                    pe.wait_ge(z_ready, CH + 1)
                    pe.wait_ge(abs_ready, CH + 1)
                for k in range(k0, k1):
                    if m == 0 and c == 0:
                        pe.wait_ge(hid_dve_ready if k % 2 else hid_ready, k // 2 + 1)
                    elif m == 0 and k < SQ1:
                        pe.wait_ge(hid_ready, HK // 2 + k + 1)
                    elif m == 0:
                        pe.wait_ge(hid_dve_ready, HK // 2 + k - SQ1 + 1)
                    last = pe.matmul(bank(VALB[c] + m), wval[:, k, m * P:(m + 1) * P],
                                     hidden[:, k, c * CT:(c + 1) * CT], start=(k == 0), stop=(k == HK - 1))
                if k1 == HK:
                    last.then_inc(val_done, 1)

            def mean3(b):
                pe.wait_ge(h2_ready, FB + b + 1)
                if b == 0:
                    pe.wait_ge(relu_ready, HK * CH)
                return half_mean(bank(MEAN3[1]), h, 1, b)

            mean2(0)
            receptance_head(1, 0)
            half_var(1, 0)
            receptance_head(1, 1)
            pe.wait_ge(v_ready, CH)
            warm(WARM2, 1)
            receptance(0)
            keys(0, 0, 6)
            wkv_out(1)
            keys(0, 6, HK)
            mean2(1)
            values(0, 0, 0, 4)
            spread_fold(bank(VAR2[1]), sq, 1, 2).then_inc(var_done, 1)
            values(0, 0, 4, HK)
            values(0, 1)
            receptance(1)
            keys(1, 0, 4)
            spread_fold(bank(MEAN3[0]), dev, 0, 3).then_inc(mean_done, 1)
            keys(1, 4, HK)
            spread_fold(bank(VAR3[0]), sq, 0, 4).then_inc(var_done, 1)
            values(1, 0)
            values(1, 1)
            mean3(0)
            weights(0, 1)
            mean3(1).then_inc(mean_done, 1)
            weights(1, 3)
            half_var(2, 1)
            weights(3, 6)

            def spread_maxima(i):
                pe.wait_ge(mx1_ready, i + 1)
                if i == 0:
                    pe.wait_ge(dev_ready, 3 * CH)
                    pe.wait_ge(ident_ready, 1)
                else:
                    pe.wait_ge(top_ready, i)
                pe.transpose(ps[:, MXB, 0:P], mx1[:, i:i + 1].to_broadcast([P, P]), ident[:, :])\
                    .then_inc(mxb_done, 1)

            def split_product(dst, w, hi, lo, ks, m, c, start, stop, lo_ready=None, count=0):
                ws, cs = slice(m * P, (m + 1) * P), slice(c * CT, (c + 1) * CT)
                for k in ks:
                    pe.matmul(dst, w[0][:, k, ws], hi[:, k, cs], start=start and k == ks[0], stop=False)
                    pe.matmul(dst, w[1][:, k, ws], hi[:, k, cs], start=False, stop=False)
                if lo_ready is not None:
                    pe.wait_ge(lo_ready, count)
                for k in ks:
                    last = pe.matmul(dst, w[0][:, k, ws], lo[:, k, cs], start=False, stop=stop and k == ks[-1])
                return last

            def expand(w, done, ready, ns, before_ready=None):
                for n in ns:
                    m, c = divmod(n, CH)
                    if 2 <= n < 6 and before_ready is None:
                        pe.wait_ge(wt_lo_ready, n + 1)
                    if n < 6 and before_ready is not None:
                        pe.wait_ge(before_ready, CH * FK - 6 + n + 1)
                    if n >= 6:
                        pe.wait_ge(ready, n - 5)
                    lo_ready = xlo_ready if m == 0 and w is wgate else None
                    if lo_ready is not None:
                        pe.wait_ge(xhi_ready, c + 1)
                    split_product(bank(TILEB[n % 6]), w, x_hi, x_lo, range(FB), m, c, True, True, lo_ready, c + 1)\
                        .then_inc(done, 1)

            pe.wait_ge(dev_ready, 3 * CH)
            pe.wait_ge(ln_ready, 4 * CH)
            warm(4, 2)
            spread_maxima(0)
            warm(WARM4, 2)
            pe.wait_ge(wt_lo_ready, 3)
            expand(wgate, gate_done, gate_ready, range(CH * FK))
            expand(wup, up_done, up_ready, range(UP_EARLY), gate_ready)
            spread_maxima(1)
            expand(wup, up_done, up_ready, range(UP_EARLY, CH * FK), gate_ready)
            spread_maxima(2)
            pe.wait_ge(up_ready, CH * FK)
            pe.wait_ge(mxsilu_ready, 4)
            warm(WARM3, 7)
            spread_maxima(3)
            weights(6, 9)
            pe.wait_ge(prod_pool_ready, 1)
            warm(WARM5, 7)
            spread_maxima(4)
            warm(WARM6, 7)

            def down(c, m, k):
                pe.wait_ge(ohi_ready, k + 1)
                pe.wait_ge(wt_lo_ready, 7 + 3 * k // FK)
                last = split_product(bank(FB * c + m), wdown, prod_hi, prod_lo, (k,), m, c, k == 0, k == FK - 1,
                                     olo_ready, k + 1)
                if k == FK - 1:
                    last.then_inc(down_done, 1)

            for k0 in (0, 2):
                for c in range(CH):
                    for k in (k0, k0 + 1):
                        for m in range(FB):
                            down(c, m, k)
            for c in range(CH):
                for m in range(FB):
                    for k in range(4, FK):
                        down(c, m, k)


def kernel(**inputs):
    import numpy as np
    import concourse.bacc as bacc
    from concourse.bass_utils import run_bass_kernel_spmd

    def inner(w):
        return w.reshape(-1, P, w.shape[1]).transpose(1, 0, 2)

    def outer(w):
        return w.reshape(-1, P, w.shape[1]).transpose(1, 0, 2).reshape(P, -1)

    g = {n: np.asarray(a) for n, a in inputs.items()}
    side = g["x"].shape[-1] // 16
    x = g["x"].reshape(IMGS, 3, side, 16, side, 16).transpose(1, 3, 5, 0, 2, 4)
    arrays = {
        "patches": x.reshape(PK, P, CH, CT).transpose(1, 2, 0, 3),
        "vecs": np.stack([g[n].reshape(FB, P) for n in VECS]).transpose(2, 0, 1),
        "wtok": inner(g["L0_tok_W"].T),
        "wk": inner(g["L0_attn_Wk"].T), "wv": inner(g["L0_attn_Wv"].T), "wr": inner(g["L0_attn_Wr"].T),
        "wo": inner(g["L0_attn_Wo"].T), "wrec": inner(g["L0_attn_Wrec"].T), "wkey": inner(g["L0_attn_Wkey"].T),
        "wval": inner(g["L0_attn_Wval"].T),
        "wgate": outer(g["L0_ffn_w_gate"]), "wup": outer(g["L0_ffn_w_up"]), "wdown": outer(g["L0_ffn_w_down"]),
    }
    nc = bacc.Bacc("TRN2", target_bir_lowering=False, num_devices=1)
    feeds, args = {}, []
    for name, a in arrays.items():
        feeds[name + "_dram"] = np.ascontiguousarray(a)
        args.append(nc.dram_tensor(name + "_dram", a.shape, mybir.dt.float32, kind="ExternalInput").ap())
    out = nc.dram_tensor("out_dram", (P, FB, NT), mybir.dt.float32, kind="ExternalOutput").ap()
    build(nc, *args, out)
    r = run_bass_kernel_spmd(nc, [feeds], core_ids=[0])
    y = r.results[0]["out_dram"].reshape(P, FB, IMGS, TOK)
    return np.ascontiguousarray(y.transpose(2, 3, 1, 0)).reshape(IMGS, TOK, D)
```
